# Optimizing a Trainium2 kernel written in Bass

```python
import numpy as np
import jax
import jax.numpy as jnp

def _softmax(x, axis=-1):
    return jax.nn.softmax(x, axis=axis)

def _gelu(x):
    return jax.nn.gelu(x, approximate=True)

def _silu(x):
    return jax.nn.silu(x)

def _sigmoid(x):
    return jax.nn.sigmoid(x)

def _layernorm(x, axis=-1, eps=1e-05):
    m = jnp.mean(x, axis=axis, keepdims=True)
    v = jnp.var(x, axis=axis, keepdims=True)
    return (x - m) / jnp.sqrt(v + eps)

def _scatter_add(tgt, idx, src, axis=0):
    return tgt.at[idx].add(src)

def _segment_sum(src, seg, n):
    return jax.ops.segment_sum(src, seg, n)
kernel_name = 'mk_gnn_resnorm_d2_gnn_r8_ac1039'

def setup_inputs(seed: int=0):
    np.random.seed(seed)
    _w = jnp.asarray

    def _rec_inputs():
        import jax
        import jax.numpy as jnp
        _gk = jax.random.key(seed)
        x = -0.0009044 + 1 * jax.random.normal(jax.random.fold_in(_gk, 1), (12500, 32), jnp.float32)
        src = jax.random.randint(jax.random.fold_in(_gk, 2), (400000,), 0, 12500, jnp.int32)
        dst = jax.random.randint(jax.random.fold_in(_gk, 3), (400000,), 0, 12500, jnp.int32)
        _o = jnp.argsort(dst, stable=True)
        src = src[_o]
        dst = dst[_o]
        edge_attr_32 = -9.77346e-05 + 0.999888 * jax.random.normal(jax.random.fold_in(_gk, 12), (400000, 32), jnp.float32)
        return (x, src, dst, edge_attr_32)
    x, src, dst, edge_attr_32 = _rec_inputs()

    def _L0_gnn_setup():
        import jax, jax.numpy as jnp
        import numpy as np
        N_NODES = 6250
        N_EDGES = 200000
        D_FEAT = 32
        key = jax.random.key(seed)
        k1, k2, k3, k4 = jax.random.split(key, 4)
        node_feat = jax.random.normal(k1, (N_NODES, D_FEAT), dtype=jnp.float32)
        edge_feat = jax.random.normal(k2, (N_EDGES, D_FEAT), dtype=jnp.float32)
        eps = jnp.zeros((1,), dtype=jnp.float32)
        src = jax.random.randint(k3, (N_EDGES,), 0, N_NODES, dtype=jnp.int64)
        dst = jax.random.randint(k4, (N_EDGES,), 0, N_NODES, dtype=jnp.int64)
        return {'node_feat': node_feat, 'edge_feat': edge_feat, 'eps': eps, 'src': src, 'dst': dst}
    _L0_gnn_all = _L0_gnn_setup()
    _L0_gnn_in = {k: v for k, v in _L0_gnn_all.items() if k in ('eps',)}
    del _L0_gnn_all

    def _L1_gnn_setup():
        import jax, jax.numpy as jnp
        import numpy as np
        N_NODES = 12500
        key = jax.random.key(seed)
        k1, k2, k3 = jax.random.split(key, 3)
        node_f = jax.random.normal(k1, (N_NODES, 32), dtype=jnp.float32)
        src = jax.random.randint(k2, (200000,), 0, N_NODES, dtype=jnp.int64)
        dst = jax.random.randint(k3, (200000,), 0, N_NODES, dtype=jnp.int64)
        return {'node_f': node_f, 'src': src, 'dst': dst}
    _L1_gnn_all = _L1_gnn_setup()
    _L1_gnn_in = {k: v for k, v in _L1_gnn_all.items() if k in ()}
    del _L1_gnn_all
    return {'x': x, 'src': src, 'dst': dst, 'edge_attr_32': edge_attr_32, 'L0_gnn_eps': _L0_gnn_in['eps']}

def reference(x, src, dst, edge_attr_32, L0_gnn_eps):
    import jax
    import jax.numpy as jnp

    def _L0_gnn_ref(node_feat, edge_feat, eps, src, dst):
        import jax, jax.numpy as jnp
        import numpy as np
        N_NODES = 6250
        N_EDGES = 200000
        D_FEAT = 32
        m = jax.nn.relu(node_feat[src] + edge_feat)
        neigh = jax.ops.segment_sum(m, dst, num_segments=node_feat.shape[0])
        return (1.0 + eps[0]) * node_feat + neigh

    def _L1_gnn_ref(node_f, src, dst):
        import jax, jax.numpy as jnp
        import numpy as np
        N_NODES = 12500
        n = node_f.shape[0]
        ones = jnp.ones(src.shape[0], dtype=node_f.dtype)
        out_deg = jnp.clip(jax.ops.segment_sum(ones, src, num_segments=n), 1.0)
        in_deg = jnp.clip(jax.ops.segment_sum(ones, dst, num_segments=n), 1.0)
        x = node_f * jax.lax.rsqrt(out_deg)[:, None]
        agg = jax.ops.segment_sum(x[src], dst, num_segments=n)
        return agg * jax.lax.rsqrt(in_deg)[:, None]
    x = _layernorm(x + _L0_gnn_ref(x, edge_attr_32, L0_gnn_eps, src, dst), axis=-1)
    x = _layernorm(x + _L1_gnn_ref(x, src, dst), axis=-1)
    return x

_drawn_inputs = setup_inputs


def setup_inputs(seed=0):
    import zlib

    import numpy as np

    out = dict(_drawn_inputs(seed))
    spreads = {}
    factors = {}
    for name, (base, spread) in spreads.items():
        noise = np.random.default_rng([zlib.crc32(name.encode()), seed]).standard_normal(out[name].shape)
        drawn = base * np.exp(spread * noise) if base else spread * noise
        out[name] = jnp.asarray(drawn.astype(out[name].dtype))
    for name, factor in factors.items():
        out[name] = (out[name] * factor).astype(out[name].dtype)
    return out
```

```python
import concourse.bass as bass
from concourse import mybir
from contextlib import ExitStack

F32, BF16, I32, U32 = mybir.dt.float32, mybir.dt.bfloat16, mybir.dt.int32, mybir.dt.uint32
ALU = mybir.AluOpType
ACT = mybir.ActivationFunctionType
AX = mybir.AxisListType

P = 128
LN_EPS = 1e-5
ROUND = 12582912.0


def build(nc, x, src, dst, edge, eps, out, table):
    N, D = x.shape
    E = src.shape[0]
    J = 25
    GE = P * J
    G = E // GE
    W = P
    C = -(-N // P)
    DE = D + 1
    TAIL = N - (P - 1) * C
    TR = 14
    assert G * GE == E and G % 2 == 1 and C % TR == 0 and TR * DE <= 512 and 0 < TAIL <= C

    with ExitStack() as ctx:
        def sb(name, shape, dt=F32):
            return ctx.enter_context(nc.sbuf_tensor(name, shape, dt))

        def pb(name, shape, dt=F32):
            return ctx.enter_context(nc.psum_tensor(name, shape, dt))

        def sem(name):
            return ctx.enter_context(nc.semaphore(name))

        src_t = sb("src_t", [P, 2, J], I32)
        dst_t = sb("dst_t", [P, 2, J], I32)
        base_t = sb("base_t", [P, 2, 1], I32)
        edge_t = sb("edge_t", [P, 2, J, D])
        rows = sb("rows", [P, 2, J, D])
        msg = sb("msg", [P, J, DE])
        rel = sb("rel", [P, J])
        quot = sb("quot", [P, J])
        s_hi = sb("s_hi", [P, J])
        s_lo = sb("s_lo", [P, J])
        dst_hot = sb("dst_hot", [P, J, W])
        hi_hot = sb("hi_hot", [P, J, P], BF16)
        lo_hot = sb("lo_hot", [P, J, C], BF16)
        iota_i = sb("iota_i", [P, P], I32)
        iota = sb("iota", [P, P])
        col_i = sb("col_i", [P, 1], I32)
        col = sb("col", [P, 1])
        ident = sb("ident", [P, P])
        zero_bf = sb("zero_bf", [P, P], BF16)
        eps_t = sb("eps_t", [P, 1])
        ln_eps = sb("ln_eps", [P, 1])
        acc = sb("acc", [DE, P * C + W])
        x_n = sb("x_n", [P, C, D])
        sums = sb("sums", [P, C, DE])
        y = sb("y", [P, C, D])
        stat = sb("stat", [P, C])
        var = sb("var", [P, C])
        rstd = sb("rstd", [P, C])
        r_out = sb("r_out", [P, C])
        r_in = sb("r_in", [P, C])
        count = sb("count", [DE, 1])
        lost = sb("lost", [DE, 1], I32)

        hist = pb("hist", [P, C])
        agg = pb("agg", [DE, W])
        turn = [pb(f"turn{k}", [P, TR * DE]) for k in range(2)]

        s_const = sem("s_const")
        s_x = sem("s_x")
        s_in = [sem(f"s_in{k}") for k in range(2)]
        s_rows = [sem(f"s_rows{k}") for k in range(2)]
        s_mark = sem("s_mark")
        s_v = sem("s_v")
        s_a = sem("s_a")
        s_agg = sem("s_agg")
        s_pe = sem("s_pe")
        s_out = sem("s_out")

        class Tally:
            def __init__(self, s):
                self.s, self.n = s, 0

            def __call__(self, ins):
                ins.then_inc(self.s, 1)
                self.n += 1
                return self.n

        V, A, PE = Tally(s_v), Tally(s_a), Tally(s_pe)

        def last_dim(ap, n):
            return ap.unsqueeze(2).to_broadcast([P, ap.shape[1], n])

        iota_j = iota[:, :].unsqueeze(1).to_broadcast([P, J, P])

        with nc.Block() as block:
            @block.gpsimd
            def _(gp):
                gp.iota(iota_i[:, :], [[1, P]], base=0, channel_multiplier=0).then_inc(s_const, 1)
                gp.iota(col_i[:, :], [[0, 1]], base=0, channel_multiplier=1).then_inc(s_const, 1)

            @block.vector
            def _(ve):
                V(ve.memset(x_n[:, :, :], 0.0))
                V(ve.memset(acc[:, :], 0.0))
                V(ve.memset(msg[:, :, D:DE], 1.0))
                V(ve.memset(zero_bf[:, :], 0.0))
                V(ve.memset(ln_eps[:, :], LN_EPS))
                ve.wait_ge(s_const, 2)
                V(ve.tensor_copy(iota[:, :], iota_i[:, :]))
                n = V(ve.tensor_copy(col[:, :], col_i[:, :]))
                ve.wait_ge(s_v, n)
                V(ve.tensor_scalar(ident[:, :], iota[:, :], col[:, 0:1], None, ALU.is_equal))

        n_const = V.n

        def load(sp, g, slot, layer):
            e0 = g * GE
            sp.dma_start(src_t[:, slot, :], src[bass.ds(e0, GE)].rearrange("(p j) -> p j", p=P)).then_inc(s_in[slot], 16)
            sp.dma_start(dst_t[:, slot, :], dst[bass.ds(e0, GE)].rearrange("(p j) -> p j", p=P)).then_inc(s_in[slot], 16)
            sp.dma_start(base_t[:, slot, :], dst[bass.ds(e0, 1)].unsqueeze(0).to_broadcast([P, 1])).then_inc(s_in[slot], 16)
            if layer == 0:
                sp.dma_start(edge_t[:, slot, :, :].rearrange("p j d -> p (j d)"),
                             edge[bass.ds(e0, GE), :].rearrange("(p j) d -> p (j d)", p=P)).then_inc(s_in[slot], 16)

        def gathers(gp, slot, nodes):
            for j in range(J):
                gp.indirect_dma_start(
                    rows[:, slot, j, :], None, nodes,
                    bass.IndirectOffsetOnAxis(ap=src_t[:, slot, j:j + 1].bitcast(U32), axis=0),
                ).then_inc(s_rows[slot], 16)

        IN = [64, 48]
        in_done = [0, 0]
        rows_done = [0, 0]
        agg_done = [0]

        def fast_pass(layer):
            nodes = (x if layer == 0 else table)[:, :]
            v0, a0, g0 = V.n, A.n, agg_done[0]
            in0, rows0 = list(in_done), list(rows_done)
            VG = 9 if layer == 0 else 3
            turns = G // 2

            def both(engine, step):
                with engine.Fori(0, turns) as i:
                    for slot in range(2):
                        step(i, slot, i * 2 + slot)
                step(turns, 0, G - 1)

            with nc.Block() as block:
                @block.sync
                def _(sp):
                    if layer == 0:
                        sp.wait_ge(s_v, 1)
                        sp.dma_start(x_n[0:P - 1, :, :], x[0:(P - 1) * C, :].rearrange("(p c) d -> p c d", c=C)).then_inc(s_x, 16)
                        sp.dma_start(x_n[P - 1:P, 0:TAIL, :], x[(P - 1) * C:N, :].unsqueeze(0)).then_inc(s_x, 16)
                        sp.dma_start(eps_t[:, :], eps.unsqueeze(0).to_broadcast([P, 1])).then_inc(s_x, 16)
                    for slot in range(2):
                        load(sp, slot, slot, layer)

                    def refill(i, slot, g):
                        if layer == 0:
                            sp.wait_ge(s_a, g + (a0 + 1))
                        else:
                            sp.wait_ge(s_agg, g + (g0 + 1))
                            sp.wait_ge(s_v, (g + 1) * VG + v0)
                        load(sp, g + 2, slot, layer)

                    with sp.Fori(0, turns - 1) as i:
                        for slot in range(2):
                            refill(i, slot, i * 2 + slot)
                    refill(turns - 1, 0, G - 3)

                @block.gpsimd
                def _(gp):
                    def step(i, slot, g):
                        gp.wait_ge(s_in[slot], (i + 1) * IN[layer] + in0[slot])
                        gp.sem_inc(s_mark, 1)
                        gathers(gp, slot, nodes)
                    both(gp, step)

                @block.vector
                def _(ve):
                    def step(i, slot, g):
                        v = g * VG + v0
                        ve.wait_ge(s_in[slot], (i + 1) * IN[layer] + in0[slot])
                        ve.tensor_scalar(rel[:, :], dst_t[:, slot, :], base_t[:, slot, 0:1], None, ALU.subtract).then_inc(s_v, 1)
                        base = ve.value_load(dst_t[0:1, slot, 0:1], min_val=0, max_val=N - 1)
                        if layer == 0:
                            ve.tensor_scalar(quot[:, :], src_t[:, slot, :], 0.5 - C / 2, 1.0 / C, ALU.add, ALU.mult).then_inc(s_v, 1)
                            ve.wait_ge(s_v, v + 2)
                            ve.tensor_scalar(s_hi[:, :], quot[:, :], ROUND, ROUND, ALU.add, ALU.subtract).then_inc(s_v, 1)
                            ve.wait_ge(s_v, v + 3)
                            ve.scalar_tensor_tensor(s_lo[:, :], s_hi[:, :], -float(C), src_t[:, slot, :], ALU.mult, ALU.add).then_inc(s_v, 1)
                            ve.tensor_tensor(hi_hot[:, :, :], iota_j, last_dim(s_hi[:, :], P), ALU.is_equal).then_inc(s_v, 1)
                            ve.wait_ge(s_v, v + 4)
                            ve.tensor_tensor(lo_hot[:, :, :], iota_j[:, :, 0:C], last_dim(s_lo[:, :], C), ALU.is_equal).then_inc(s_v, 1)
                        else:
                            ve.wait_ge(s_v, v + 1)
                        ve.tensor_tensor(dst_hot[:, :, :], iota_j, last_dim(rel[:, :], W), ALU.is_equal).then_inc(s_v, 1)
                        if layer == 0:
                            ve.wait_ge(s_rows[slot], (i + 1) * 16 * J + rows0[slot])
                            ve.tensor_tensor(edge_t[:, slot, :, :], edge_t[:, slot, :, :], rows[:, slot, :, :], ALU.add).then_inc(s_v, 1)
                        M = DE if layer == 0 else D
                        ve.wait_ge(s_agg, g + (g0 + 1))
                        window = acc[0:M, bass.ds(base, W)]
                        ve.tensor_tensor(window, window, agg[0:M, :], ALU.add).then_inc(s_v, 1)
                    both(ve, step)

                if layer == 0:
                    @block.scalar
                    def _(sc):
                        def step(i, slot, g):
                            sc.wait_ge(s_v, g * VG + (v0 + 8))
                            sc.activation(msg[:, :, 0:D], edge_t[:, slot, :, :], ACT.Relu).then_inc(s_a, 1)
                        both(sc, step)

                @block.tensor
                def _(te):
                    if layer == 0:
                        te.wait_ge(s_v, n_const)
                        te.matmul(hist[:, :], zero_bf[:, :], zero_bf[:, 0:C], start=True, stop=False)

                    def step(i, slot, g):
                        v = g * VG + v0
                        if layer == 0:
                            te.wait_ge(s_v, v + 6)
                            for j in range(J):
                                te.matmul(hist[:, :], hi_hot[:, j, :], lo_hot[:, j, :], start=False, stop=False)
                            te.wait_ge(s_a, g + (a0 + 1))
                        else:
                            te.wait_ge(s_rows[slot], (i + 1) * 16 * J + rows0[slot])
                            te.wait_ge(s_v, v + 2)
                        for j in range(J):
                            lhs = msg[:, j, :] if layer == 0 else rows[:, slot, j, :]
                            M = DE if layer == 0 else D
                            last = te.matmul(agg[0:M, :], lhs, dst_hot[:, j, :], start=(j == 0), stop=(j == J - 1))
                        last.then_inc(s_agg, 1)
                    both(te, step)
                    if layer == 0:
                        PE(te.matmul(hist[:, :], zero_bf[:, :], zero_bf[:, 0:C], start=False, stop=True))

            V.n += VG * G
            A.n += G if layer == 0 else 0
            agg_done[0] += G
            for slot in range(2):
                uses = (G + 1 - slot) // 2
                in_done[slot] += IN[layer] * uses
                rows_done[slot] += 16 * J * uses

        def count_edges():
            v0, p0 = V.n, PE.n
            with nc.Block() as block:
                @block.vector
                def _(ve):
                    n = V(ve.tensor_reduce(count[D:DE, :], acc[D:DE, 0:P * C], AX.X, ALU.add))
                    ve.wait_ge(s_v, n)
                    V(ve.tensor_scalar(lost[D:DE, :], count[D:DE, :], float(E), None, ALU.not_equal))

        def general_sums(layer):
            nodes = (x if layer == 0 else table)[:, :]
            M = DE if layer == 0 else D
            v0 = V.n
            g_in, g_rows, g_v, g_a, g_pe = (sem(f"g_{what}{layer}") for what in ("in", "rows", "v", "a", "pe"))
            B = 2 if layer == 0 else 1
            VT = B + 3 * C
            with nc.Block() as block:
                def when_lost(engine):
                    engine.wait_ge(s_v, v0)
                    return engine.If(engine.value_load(lost[D:DE, 0:1], min_val=0, max_val=1) > 0)

                @block.sync
                def _(sp):
                    with when_lost(sp):
                        with sp.Fori(0, G) as g:
                            sp.wait_ge(g_v, g * VT + 1)
                            e0 = g * GE
                            sp.dma_start(src_t[:, 0, :], src[bass.ds(e0, GE)].rearrange("(p j) -> p j", p=P)).then_inc(g_in, 16)
                            sp.dma_start(dst_t[:, 0, :], dst[bass.ds(e0, GE)].rearrange("(p j) -> p j", p=P)).then_inc(g_in, 16)
                            sp.dma_start(edge_t[:, 0, :, :].rearrange("p j d -> p (j d)"),
                                         edge[bass.ds(e0, GE), :].rearrange("(p j) d -> p (j d)", p=P)).then_inc(g_in, 16)

                @block.gpsimd
                def _(gp):
                    with when_lost(gp):
                        with gp.Fori(0, G) as g:
                            gp.wait_ge(g_in, (g + 1) * 48)
                            gp.sem_inc(s_mark, 1)
                            for j in range(J):
                                gp.indirect_dma_start(
                                    rows[:, 0, j, :], None, nodes,
                                    bass.IndirectOffsetOnAxis(ap=src_t[:, 0, j:j + 1].bitcast(U32), axis=0),
                                ).then_inc(g_rows, 16)

                @block.vector
                def _(ve):
                    with when_lost(ve):
                        ve.memset(acc[:, :], 0.0).then_inc(g_v, 1)
                        with ve.Fori(0, G) as g:
                            v = g * VT + 1
                            ve.wait_ge(g_in, (g + 1) * 48)
                            ve.tensor_copy(rel[:, :], dst_t[:, 0, :]).then_inc(g_v, 1)
                            if layer == 0:
                                ve.wait_ge(g_rows, (g + 1) * (16 * J))
                                ve.tensor_tensor(edge_t[:, 0, :, :], edge_t[:, 0, :, :], rows[:, 0, :, :], ALU.add).then_inc(g_v, 1)
                            with ve.Fori(0, C) as w:
                                u = v + B + w * 3
                                ve.wait_ge(g_v, u)
                                ve.tensor_tensor(dst_hot[:, :, :], iota_j, last_dim(rel[:, :], W), ALU.is_equal).then_inc(g_v, 1)
                                ve.wait_ge(g_v, u + 1)
                                ve.tensor_scalar(rel[:, :], rel[:, :], float(W), None, ALU.subtract).then_inc(g_v, 1)
                                ve.wait_ge(g_pe, g * C + w + 1)
                                window = acc[0:M, bass.ds(w * W, W)]
                                ve.tensor_tensor(window, window, agg[0:M, :], ALU.add).then_inc(g_v, 1)

                if layer == 0:
                    @block.scalar
                    def _(sc):
                        with when_lost(sc):
                            with sc.Fori(0, G) as g:
                                sc.wait_ge(g_v, g * VT + 3)
                                sc.activation(msg[:, :, 0:D], edge_t[:, 0, :, :], ACT.Relu).then_inc(g_a, 1)

                @block.tensor
                def _(te):
                    with when_lost(te):
                        with te.Fori(0, G) as g:
                            if layer == 0:
                                te.wait_ge(g_a, g + 1)
                            else:
                                te.wait_ge(g_rows, (g + 1) * (16 * J))
                            te.sem_inc(s_mark, 1)
                            with te.Fori(0, C) as w:
                                te.wait_ge(g_v, g * VT + w * 3 + (B + 2))
                                for j in range(J):
                                    lhs = msg[:, j, :] if layer == 0 else rows[:, 0, j, :]
                                    last = te.matmul(agg[0:M, :], lhs, dst_hot[:, j, :], start=(j == 0), stop=(j == J - 1))
                                last.then_inc(g_pe, 1)

        def to_nodes(layer):
            M = DE if layer == 0 else D
            v0, p0 = V.n, PE.n
            with nc.Block() as block:
                @block.tensor
                def _(te):
                    for k in range(C // TR):
                        if k >= 2:
                            te.wait_ge(s_v, v0 + k - 1)
                        for t in range(TR):
                            c = k * TR + t
                            last = te.matmul(turn[k % 2][:, t * M:(t + 1) * M], acc[0:M, c:c + (P - 1) * C + 1:C],
                                             ident[0:M, 0:M], start=True, stop=True)
                        PE(last)

                @block.vector
                def _(ve):
                    for k in range(C // TR):
                        ve.wait_ge(s_pe, p0 + k + 1)
                        V(ve.tensor_copy(sums[:, k * TR:(k + 1) * TR, 0:M],
                                         turn[k % 2][:, 0:TR * M].rearrange("p (t m) -> p t m", m=M)))

        def wide(ap):
            return ap.unsqueeze(2).to_broadcast([P, C, D])

        def finish(layer):
            v0, a0 = V.n, A.n
            ve_steps, sc_steps = [], []
            with nc.Block() as block:
                @block.vector
                def _(ve):
                    a = [a0]

                    def after(ins):
                        ve.wait_ge(s_v, V(ins))

                    def scalar_step(make):
                        sc_steps.append((V.n, make))
                        a[0] += 1
                        ve.wait_ge(s_a, a[0])

                    agg_n = sums[:, :, 0:D]
                    if layer == 0:
                        ve.wait_ge(s_x, 48)
                        after(ve.tensor_scalar(eps_t[:, :], eps_t[:, :], 1.0, None, ALU.add))
                        after(ve.scalar_tensor_tensor(y[:, :, :], x_n[:, :, :], eps_t[:, 0:1], agg_n, ALU.mult, ALU.add))
                        after(ve.tensor_tensor(y[:, :, :], y[:, :, :], x_n[:, :, :], ALU.add))
                        after(ve.tensor_scalar(r_out[:, :], hist[:, :], 1.0, None, ALU.max))
                        after(ve.tensor_scalar(r_in[:, :], sums[:, :, D], 1.0, None, ALU.max))
                        scalar_step(lambda sc: sc.activation(r_out[:, :], r_out[:, :], ACT.Sqrt))
                        scalar_step(lambda sc: sc.activation(r_in[:, :], r_in[:, :], ACT.Sqrt))
                        after(ve.reciprocal(r_out[:, :], r_out[:, :]))
                        after(ve.reciprocal(r_in[:, :], r_in[:, :]))
                    else:
                        after(ve.tensor_tensor(y[:, :, :], agg_n, wide(r_in[:, :]), ALU.mult))
                        after(ve.tensor_tensor(y[:, :, :], y[:, :, :], x_n[:, :, :], ALU.add))
                    after(ve.tensor_reduce(stat[:, :], y[:, :, :], AX.X, ALU.add))
                    after(ve.tensor_scalar(stat[:, :], stat[:, :], 1.0 / D, None, ALU.mult))
                    after(ve.tensor_tensor(y[:, :, :], y[:, :, :], wide(stat[:, :]), ALU.subtract))
                    after(ve.tensor_tensor(agg_n, y[:, :, :], y[:, :, :], ALU.mult))
                    after(ve.tensor_reduce(var[:, :], agg_n, AX.X, ALU.add))
                    scalar_step(lambda sc: sc.activation(rstd[:, :], var[:, :], ACT.Sqrt, bias=ln_eps[:, 0:1], scale=1.0 / D))
                    after(ve.reciprocal(rstd[:, :], rstd[:, :]))
                    after(ve.tensor_tensor(x_n[:, :, :], y[:, :, :], wide(rstd[:, :]), ALU.mult))
                    if layer == 0:
                        after(ve.tensor_tensor(y[:, :, :], x_n[:, :, :], wide(r_out[:, :]), ALU.mult))
                        after(ve.memset(acc[:, :], 0.0))
                v_done = V.n

                @block.scalar
                def _(sc):
                    for n, make in sc_steps:
                        sc.wait_ge(s_v, n)
                        A(make(sc))

                @block.sync
                def _(sp):
                    if layer == 0:
                        sp.wait_ge(s_v, v_done - 1)
                        sp.dma_start(table.rearrange("(p c) d -> p c d", c=C), y[:, :, :]).then_inc(s_out, 16)
                        sp.wait_ge(s_out, 16)
                    else:
                        sp.wait_ge(s_v, v_done)
                        sp.dma_start(out[0:(P - 1) * C, :].rearrange("(p c) d -> p c d", c=C), x_n[0:P - 1, :, :]).then_inc(s_out, 16)
                        sp.dma_start(out[(P - 1) * C:N, :].unsqueeze(0), x_n[P - 1:P, 0:TAIL, :]).then_inc(s_out, 16)
                        sp.wait_ge(s_out, 48)

        fast_pass(0)
        count_edges()
        general_sums(0)
        to_nodes(0)
        finish(0)
        fast_pass(1)
        general_sums(1)
        to_nodes(1)
        finish(1)


_INS = ['x', 'src', 'dst', 'edge_attr_32', 'L0_gnn_eps']


def kernel(**inputs):
    import numpy as _np
    import concourse.bacc as _bacc
    from concourse import mybir as _mybir
    from concourse.bass_utils import run_bass_kernel_spmd as _run

    nc = _bacc.Bacc("TRN2", target_bir_lowering=False, num_devices=1)
    arrays, args = {}, []
    for name in _INS:
        a = _np.ascontiguousarray(inputs[name])
        arrays[f"in_{name}"] = a
        args.append(nc.dram_tensor(f"in_{name}", a.shape, _mybir.dt.from_np(a.dtype), kind="ExternalInput").ap())
    n, d = inputs['x'].shape
    out = nc.dram_tensor("out", (n, d), _mybir.dt.float32, kind="ExternalOutput").ap()
    table = nc.dram_tensor("table", (-(-n // 128) * 128, d), _mybir.dt.float32, kind="Internal").ap()
    build(nc, *args, out, table)
    r = _run(nc, [arrays], core_ids=[0])
    return r.results[0]["out"]
```

```python
import concourse.bass as bass
from concourse import mybir
from contextlib import ExitStack

F32, BF16, F16, I32, U32 = mybir.dt.float32, mybir.dt.bfloat16, mybir.dt.float16, mybir.dt.int32, mybir.dt.uint32
ALU = mybir.AluOpType
ACT = mybir.ActivationFunctionType
AX = mybir.AxisListType

P = 128
PARTS = 3
SPAN = 8
LN_EPS = 1e-5
ROUND = 12582912.0


def build(nc, x, src, dst, edge, eps, out, table, x1):
    N, D = x.shape
    E = src.shape[0]
    J = 25
    GE = P * J
    G = E // GE
    W = P
    C = -(-N // P)
    DE = D + 1
    D3 = PARTS * D
    TAIL = N - (P - 1) * C
    TR = 14
    NC = G // 2
    NG = G - NC
    CE0 = NG * GE
    KEYS = C * SPAN
    HK = KEYS // 2
    CH = 5
    HT = [13, J - 13]
    HS = [n * SPAN for n in HT]
    STEPS = -(-C // J)
    assert G * GE == E and G % 2 == 1 and NC % 2 == 0 and NG == NC + 1 and NC <= P
    assert C % TR == 0 and TR * DE <= 512 and 0 < TAIL <= C and HK <= 512 and max(HS) <= P and J % CH == 0

    with ExitStack() as ctx:
        def allocators(stack):
            return (lambda name, shape, dt=F32: stack.enter_context(nc.sbuf_tensor(name, shape, dt)),
                    lambda name: stack.enter_context(nc.psum_tensor(name, [P, 512], F32)))

        sb, pb = allocators(ctx)

        def sem(name):
            return ctx.enter_context(nc.semaphore(name))

        iota_i = sb("iota_i", [P, P], I32)
        iota = sb("iota", [P, P])
        iota_b = sb("iota_b", [P, P], BF16)
        col_i = sb("col_i", [P, 1], I32)
        col = sb("col", [P, 1])
        low_i = sb("low_i", [P, 2], I32)
        low = sb("low", [P, 2])
        ident = sb("ident", [P, P])
        fold = sb("fold", [D3, D])
        ones = sb("ones", [P, 1])
        zero_bf = sb("zero_bf", [P, P], BF16)
        eps_t = sb("eps_t", [P, 1])
        ln_eps = sb("ln_eps", [P, 1])
        acc = sb("acc", [D3, P * C + W])
        r_out = sb("r_out", [P, C])
        r_in = sb("r_in", [P, C])
        x_parts = sb("x_parts", [P, C, D3], BF16)
        hi_all = sb("hi_all", [P, J, NC])
        key_all = sb("key_all", [P, J, NC])
        first_i = sb("first_i", [J, NC], I32)
        place = sb("place", [max(HS), 2, NC])
        count = sb("count", [DE, 1])
        lost = sb("lost", [DE, 1], I32)
        lost1 = sb("lost1", [1, 1], I32)

        s_const = sem("s_const")
        s_x = sem("s_x")
        s_prep = sem("s_prep")
        s_in = [sem(f"s_in{k}") for k in range(2)]
        s_rows = [sem(f"s_rows{k}") for k in range(2)]
        s_mark = sem("s_mark")
        s_v = sem("s_v")
        s_a = sem("s_a")
        s_pe = sem("s_pe")
        s_agg = sem("s_agg")
        s_out = sem("s_out")

        class Tally:
            def __init__(self, s):
                self.s, self.n = s, 0

            def __call__(self, ins):
                ins.then_inc(self.s, 1)
                self.n += 1
                return self.n

        V, A, PE = Tally(s_v), Tally(s_a), Tally(s_pe)

        def last_dim(ap, n):
            return ap.unsqueeze(2).to_broadcast([ap.shape[0], ap.shape[1], n])

        def tiles_of(ap, n):
            return ap.unsqueeze(1).to_broadcast([P, n, P])

        def load_indices(sp, g, src_d, dst_d, base_d, s):
            e0 = g * GE
            sp.dma_start(src_d, src[bass.ds(e0, GE)].rearrange("(p j) -> p j", p=P)).then_inc(s, 16)
            sp.dma_start(dst_d, dst[bass.ds(e0, GE)].rearrange("(p j) -> p j", p=P)).then_inc(s, 16)
            if base_d is not None:
                sp.dma_start(base_d, dst[bass.ds(e0, 1)].unsqueeze(0).to_broadcast([P, 1])).then_inc(s, 16)

        def load_edges(sp, g, edge_d, s):
            e0 = g * GE
            sp.dma_start(edge_d.rearrange("p j d -> p (j d)"),
                         edge[bass.ds(e0, GE), :].rearrange("(p j) d -> p (j d)", p=P)).then_inc(s, 16)

        def gathers(gp, nodes, rows_d, src_d, s):
            for j in range(J):
                gp.indirect_dma_start(
                    rows_d[:, j, :], None, nodes,
                    bass.IndirectOffsetOnAxis(ap=src_d[:, j:j + 1].bitcast(U32), axis=0),
                ).then_inc(s, 16)

        with nc.Block() as block:
            @block.gpsimd
            def _(gp):
                gp.iota(iota_i[:, :], [[1, P]], base=0, channel_multiplier=0).then_inc(s_const, 1)
                gp.iota(col_i[:, :], [[0, 1]], base=0, channel_multiplier=1).then_inc(s_const, 1)

            @block.vector
            def _(ve):
                V(ve.memset(zero_bf[:, :], 0.0))
                V(ve.memset(ones[:, :], 1.0))
                V(ve.memset(ln_eps[:, :], LN_EPS))
                ve.wait_ge(s_const, 2)
                V(ve.tensor_copy(iota[:, :], iota_i[:, :]))
                V(ve.tensor_copy(iota_b[:, :], iota_i[:, :]))
                V(ve.tensor_copy(col[:, :], col_i[:, :]))
                V(ve.tensor_scalar(low_i[:, 0:1], col_i[:, :], D - 1, None, ALU.bitwise_and))
                n = V(ve.tensor_scalar(low_i[:, 1:2], col_i[:, :], SPAN - 1, None, ALU.bitwise_and))
                ve.wait_ge(s_v, n)
                V(ve.tensor_scalar(ident[:, :], iota[:, :], col[:, 0:1], None, ALU.is_equal))
                n = V(ve.tensor_copy(low[:, :], low_i[:, :]))
                ve.wait_ge(s_v, n)
                V(ve.tensor_scalar(fold[:, :], iota[0:D3, 0:D], low[0:D3, 0:1], None, ALU.is_equal))
                V(ve.memset(acc[:, :], 0.0))
        n_const = V.n

        def layer_0():
            turns = G // 2

            def both(engine, step):
                with engine.Fori(0, turns) as i:
                    for slot in range(2):
                        step(i, slot, i * 2 + slot)
                step(turns, 0, G - 1)

            with ExitStack() as own:
                sb, pb = allocators(own)
                src_t = sb("src_t", [P, 2, J], I32)
                dst_t = sb("dst_t", [P, 2, J], I32)
                base_t = sb("base_t", [P, 2, 1], I32)
                edge_t = sb("edge_t", [P, 2, J, D])
                rows = sb("rows", [P, 2, J, D])
                msg = sb("msg", [P, J, DE])
                rel = sb("rel", [P, J])
                quot = sb("quot", [P, J])
                s_hi = sb("s_hi", [P, J])
                s_lo = sb("s_lo", [P, J])
                dst_hot = sb("dst_hot", [P, J, W])
                hi_hot = sb("hi_hot", [P, J, P], BF16)
                lo_hot = sb("lo_hot", [P, J, C], BF16)
                c_dst = sb("c_dst", [NC, J, P], I32)
                c_src = sb("c_src", [NC, J, P], I32)
                c_rel = sb("c_rel", [NC, J, P])
                c_hi = sb("c_hi", [NC, J, P])
                c_key = c_src[:, :, :].bitcast(F32)
                first = sb("first", [J, NC])
                pick_i = sb("pick_i", [J, 2, max(HS)], I32)
                pick = sb("pick", [J, 2, max(HS)])
                is_0 = sb("is_0", [J, 1])
                most = sb("most", [NC, 2])
                bad = sb("bad", [NC, 1])
                agg = pb("agg")[0:DE, 0:W]
                turn = [pb(f"turn{k}") for k in range(2)]
                misc = pb("misc")

                VG = 9

                TB = 8
                ROUNDS = [(what, t, min(TB, J - t)) for what in range(2) for t in range(0, J, TB)]

                def prepare_dve(ve):
                    def after(ins):
                        ve.wait_ge(s_v, V(ins))
                    V(ve.memset(msg[:, :, D:DE], 1.0))
                    ve.wait_ge(s_prep, 48)
                    V(ve.tensor_tensor(c_rel[:, :, :], c_dst[:, :, :], c_dst[:, :, 0:1].to_broadcast([NC, J, P]), ALU.subtract))
                    after(ve.tensor_scalar(c_hi[:, :, :], c_src[:, :, :], 0.5 - C / 2, 1.0 / C, ALU.add, ALU.mult))
                    after(ve.tensor_scalar(c_hi[:, :, :], c_hi[:, :, :], ROUND, ROUND, ALU.add, ALU.subtract))
                    after(ve.scalar_tensor_tensor(c_key, c_hi[:, :, :], -float(C), c_src[:, :, :], ALU.mult, ALU.add))
                    after(ve.scalar_tensor_tensor(c_key, c_key, float(SPAN), c_rel[:, :, :], ALU.mult, ALU.add))
                    n_keys = V.n
                    ve.wait_ge(s_const, 4)
                    V(ve.tensor_copy(first[:, :], first_i[:, :]))
                    V(ve.tensor_scalar(is_0[:, :], col[0:J, :], 0.0, None, ALU.is_equal))
                    after(ve.tensor_scalar(pick[:, :, :], pick_i[:, :, :], col[0:J, 0:1], None, ALU.is_equal))
                    after(ve.tensor_scalar(pick[:, :, :], pick[:, :, :], is_0[:, 0:1], None, ALU.subtract))
                    n_pick = V.n
                    V(ve.tensor_reduce(most[:, 0:1], c_rel[:, :, :], AX.XY, ALU.max))
                    after(ve.tensor_reduce(most[:, 1:2], c_rel[:, :, :], AX.XY, ALU.min))
                    after(ve.tensor_scalar(bad[:, :], most[:, 0:1], float(SPAN - 1), None, ALU.is_gt))
                    after(ve.scalar_tensor_tensor(bad[:, :], most[:, 1:2], 0.0, bad[:, :], ALU.is_lt, ALU.add))
                    n_bad = V.n
                    for k, (what, t, m) in enumerate(ROUNDS):
                        ve.wait_ge(s_pe, k + 1)
                        V(ve.tensor_copy((hi_all, key_all)[what][:, t:t + m, :],
                                         turn[k % 2][:, 0:m * NC].rearrange("p (t g) -> p t g", g=NC)))
                    ve.wait_ge(s_pe, len(ROUNDS) + 1)
                    for h in range(2):
                        V(ve.tensor_scalar(place[0:HS[h], h, :], misc[0:HS[h], h * NC:(h + 1) * NC], low[0:HS[h], 1:2], None, ALU.add))
                    V(ve.tensor_scalar(lost1[:, :], misc[0:1, 2 * NC:2 * NC + 1], 0.0, None, ALU.is_gt))
                    return n_keys, n_pick, n_bad

                def prepare_pe(te):
                    te.wait_ge(s_v, n_keys)
                    for k, (what, t, m) in enumerate(ROUNDS):
                        if k >= 2:
                            te.wait_ge(s_v, n_bad + k - 1)
                        for q in range(m):
                            turned = (c_hi[:, :, :], c_key)[what][:, t + q, :]
                            last = te.matmul(turn[k % 2][:, q * NC:(q + 1) * NC], turned, ident[0:NC, 0:NC], start=True, stop=True)
                        PE(last)
                    te.wait_ge(s_v, n_bad)
                    for h in range(2):
                        te.matmul(misc[0:HS[h], h * NC:(h + 1) * NC], pick[:, h, 0:HS[h]], first[:, :], start=True, stop=True)
                    PE(te.matmul(misc[0:1, 2 * NC:2 * NC + 1], bad[:, :], ones[0:NC, :], start=True, stop=True))

                with nc.Block() as block:
                    @block.vector
                    def _(ve):
                        nonlocal n_keys, n_bad, v0
                        n_keys, _, n_bad = prepare_dve(ve)
                        v0 = V.n

                        def step(i, slot, g):
                            v = g * VG + v0
                            ve.wait_ge(s_in[slot], (i + 1) * 64)
                            ve.tensor_scalar(rel[:, :], dst_t[:, slot, :], base_t[:, slot, 0:1], None, ALU.subtract).then_inc(s_v, 1)
                            base = ve.value_load(dst_t[0:1, slot, 0:1], min_val=0, max_val=N - 1)
                            ve.tensor_scalar(quot[:, :], src_t[:, slot, :], 0.5 - C / 2, 1.0 / C, ALU.add, ALU.mult).then_inc(s_v, 1)
                            ve.wait_ge(s_v, v + 2)
                            ve.tensor_scalar(s_hi[:, :], quot[:, :], ROUND, ROUND, ALU.add, ALU.subtract).then_inc(s_v, 1)
                            ve.wait_ge(s_v, v + 3)
                            ve.scalar_tensor_tensor(s_lo[:, :], s_hi[:, :], -float(C), src_t[:, slot, :], ALU.mult, ALU.add).then_inc(s_v, 1)
                            ve.tensor_tensor(hi_hot[:, :, :], tiles_of(iota[:, :], J), last_dim(s_hi[:, :], P), ALU.is_equal).then_inc(s_v, 1)
                            ve.wait_ge(s_v, v + 4)
                            ve.tensor_tensor(lo_hot[:, :, :], tiles_of(iota[:, :], J)[:, :, 0:C], last_dim(s_lo[:, :], C), ALU.is_equal).then_inc(s_v, 1)
                            ve.tensor_tensor(dst_hot[:, :, :], tiles_of(iota[:, :], J), last_dim(rel[:, :], W), ALU.is_equal).then_inc(s_v, 1)
                            ve.wait_ge(s_rows[slot], (i + 1) * (16 * J))
                            ve.tensor_tensor(edge_t[:, slot, :, :], edge_t[:, slot, :, :], rows[:, slot, :, :], ALU.add).then_inc(s_v, 1)
                            ve.wait_ge(s_agg, g + 1)
                            window = acc[0:DE, bass.ds(base, W)]
                            ve.tensor_tensor(window, window, agg[:, :], ALU.add).then_inc(s_v, 1)
                        both(ve, step)

                    @block.sync
                    def _(sp):
                        def load(g, slot):
                            load_indices(sp, g, src_t[:, slot, :], dst_t[:, slot, :], base_t[:, slot, :], s_in[slot])
                            load_edges(sp, g, edge_t[:, slot, :, :], s_in[slot])

                        for slot in range(2):
                            load(slot, slot)
                        sp.dma_start(c_dst[:, :, :].rearrange("g j p -> g (j p)"), dst[CE0:E].rearrange("(g e) -> g e", e=GE)).then_inc(s_prep, 16)
                        sp.dma_start(c_src[:, :, :].rearrange("g j p -> g (j p)"), src[CE0:E].rearrange("(g e) -> g e", e=GE)).then_inc(s_prep, 16)
                        with nc.allow_non_contiguous_dma(reason="one index of each tile, once"):
                            sp.dma_start(first_i[:, :], dst[CE0:E].rearrange("(g j p) -> j g p", p=P, j=J)[:, :, 0]).then_inc(s_prep, 16)
                        sp.dma_start(eps_t[:, :], eps.unsqueeze(0).to_broadcast([P, 1])).then_inc(s_x, 16)

                        def refill(i, slot, g):
                            sp.wait_ge(s_a, g + 1)
                            load(g + 2, slot)
                        with sp.Fori(0, turns - 1) as i:
                            for slot in range(2):
                                refill(i, slot, i * 2 + slot)
                        refill(turns - 1, 0, G - 3)

                    @block.gpsimd
                    def _(gp):
                        for h in range(2):
                            gp.iota(pick_i[:, h, :], [[1, max(HT)], [0, SPAN]], base=h * HT[0], channel_multiplier=0).then_inc(s_const, 1)

                        def step(i, slot, g):
                            gp.wait_ge(s_in[slot], (i + 1) * 64)
                            gp.sem_inc(s_mark, 1)
                            gathers(gp, x[:, :], rows[:, slot, :, :], src_t[:, slot, :], s_rows[slot])
                        both(gp, step)

                    @block.scalar
                    def _(sc):
                        def step(i, slot, g):
                            sc.wait_ge(s_v, g * VG + (v0 + 8))
                            sc.activation(msg[:, :, 0:D], edge_t[:, slot, :, :], ACT.Relu).then_inc(s_a, 1)
                        both(sc, step)

                    @block.tensor
                    def _(te):
                        te.wait_ge(s_v, n_const)
                        te.matmul(hist[:, :], zero_bf[:, :], zero_bf[:, 0:C], start=True, stop=False)
                        prepare_pe(te)

                        def step(i, slot, g):
                            te.wait_ge(s_v, g * VG + (v0 + 6))
                            for j in range(J):
                                te.matmul(hist[:, :], hi_hot[:, j, :], lo_hot[:, j, :], start=False, stop=False)
                            te.wait_ge(s_a, g + 1)
                            for j in range(J):
                                last = te.matmul(agg[:, :], msg[:, j, :], dst_hot[:, j, :], start=(j == 0), stop=(j == J - 1))
                            last.then_inc(s_agg, 1)
                        both(te, step)
                        PE(te.matmul(hist[:, :], zero_bf[:, :], zero_bf[:, 0:C], start=False, stop=True))

                V.n += VG * G
                A.n += G
                with nc.Block() as block:
                    @block.vector
                    def _(ve):
                        n = V(ve.tensor_reduce(count[D:DE, :], acc[D:DE, 0:P * C], AX.X, ALU.add))
                        ve.wait_ge(s_v, n)
                        V(ve.tensor_scalar(lost[D:DE, :], count[D:DE, :], float(E), None, ALU.not_equal))
                general_sums(0, x[:, :], DE, (src_t, dst_t, rows, rel, dst_hot, agg), edge_t, msg)

        n_keys = n_bad = v0 = 0

        def layer_1():
            LAST = NC + 1

            def each(engine, step, last):
                step(0, 0, 0)
                step(1, 1, 0)
                with engine.Fori(0, NC // 2 - 1) as i:
                    for slot in range(2):
                        step(i * 2 + (2 + slot), slot, i + 1)
                for k in range(NC, last + 1):
                    step(k, k % 2, k // 2)

            def within(k, lo, hi):
                return not isinstance(k, int) or lo <= k <= hi

            with ExitStack() as own:
                sb, pb = allocators(own)
                src_t = sb("src_1", [P, 2, J], I32)
                dst_t = sb("dst_1", [P, 2, J], I32)
                base_t = sb("base_1", [P, 2, 1], I32)
                rows = sb("rows_1", [P, 2, J, D3], BF16)
                rel = sb("rel_1", [P, J])
                dst_hot = sb("dst_hot_1", [P, J, W], BF16)
                hi_g = sb("hi_g", [P, J])
                key_g = sb("key_g", [P, J])
                hi_hot = sb("hi_hot_1", [P, 2, CH, P], BF16)
                key_hot = sb("key_hot", [P, 2, CH, KEYS], BF16)
                counts = sb("counts", [P, 2, C, J * SPAN], BF16)
                prod = sb("prod", [D3, J * SPAN])
                slots = sb("slots", [max(HS), 2, D])
                place_hot = sb("place_hot", [max(HS), 2, W])
                built = [own.enter_context(nc.psum_tensor(f"built{k}", [P, 2, 512], F32)) for k in range(2)]
                applied = pb("applied")[0:D3, 0:J * SPAN]
                agg = pb("agg_1")[0:D3, 0:W]
                small = pb("small")
                slot_ps = small[0:max(HS), 0:2 * D]
                put = small[0:D, 2 * D:2 * D + W]
                key_iota = sb("key_iota", [P, KEYS], F16)[:, :]

                l_in = [sem(f"l_in{k}") for k in range(2)]
                l_rows = [sem(f"l_rows{k}") for k in range(2)]
                l_hot = sem("l_hot")
                l_rel = sem("l_rel")
                l_keys = sem("l_keys")
                l_chunk = sem("l_chunk")
                l_place = sem("l_place")
                l_acc = sem("l_acc")
                l_sum = sem("l_sum")
                l_built = sem("l_built")
                l_applied = sem("l_applied")
                l_slot = sem("l_slot")
                l_put = sem("l_put")
                l_counts = sem("l_counts")
                l_prod = sem("l_prod")
                l_iota = sem("l_iota")

                with nc.Block() as block:
                    @block.gpsimd
                    def _(gp):
                        gp.iota(counts[:, 0, 0:SPAN, :].rearrange("p a b -> p (a b)")[:, 0:2 * KEYS].bitcast(I32),
                                [[1, KEYS]], base=0, channel_multiplier=0).then_inc(l_iota, 1)

                    @block.vector
                    def _(ve):
                        ve.wait_ge(l_iota, 1)
                        ve.tensor_copy(key_iota, counts[:, 0, 0:SPAN, :].rearrange("p a b -> p (a b)")[:, 0:2 * KEYS].bitcast(I32)).then_inc(l_iota, 1)
                        ve.wait_ge(l_iota, 2)

                with nc.Block() as block:
                    @block.sync
                    def _(sp):
                        def step(g, slot, use):
                            if within(g, 2, NG):
                                sp.wait_ge(l_rows[slot], use * (16 * J))
                                sp.wait_ge(l_hot, g - 1)
                            load_indices(sp, g, src_t[:, slot, :], dst_t[:, slot, :], base_t[:, slot, :], l_in[slot])
                        each(sp, step, NG - 1)

                    @block.gpsimd
                    def _(gp):
                        def step(g, slot, use):
                            gp.wait_ge(l_in[slot], (use + 1) * 48)
                            gp.sem_inc(s_mark, 1)
                            if within(g, 2, NG):
                                gp.wait_ge(l_sum, g - 1)
                                gp.sem_inc(s_mark, 1)
                            gathers(gp, table[:, :], rows[:, slot, :, :], src_t[:, slot, :], l_rows[slot])
                        each(gp, step, NG - 1)

                    @block.vector
                    def _(ve):
                        def step(k, slot, use):
                            other = 1 - slot
                            other_use = use + slot
                            gathered = within(k, 1, NG)
                            building = within(k, 0, NC - 1)
                            placing = within(k, 2, NC + 1)
                            if gathered:
                                ve.wait_ge(l_in[other], other_use * 48)
                                ve.tensor_scalar(rel[:, :], dst_t[:, other, :], base_t[:, other, 0:1], None, ALU.subtract).then_inc(l_rel, 1)
                                base = ve.value_load(dst_t[0:1, other, 0:1], min_val=0, max_val=N - 1)
                                if within(k, 2, NG):
                                    ve.wait_ge(l_sum, k - 1)
                                ve.wait_ge(l_rel, k)
                                ve.tensor_tensor(dst_hot[:, :, :], tiles_of(iota_b[:, :], J), last_dim(rel[:, :], W), ALU.is_equal).then_inc(l_hot, 1)
                            if building:
                                ve.tensor_copy(hi_g[:, :], hi_all[:, :, bass.ds(k, 1)].squeeze(2)).then_inc(l_keys, 1)
                                ve.tensor_copy(key_g[:, :], key_all[:, :, bass.ds(k, 1)].squeeze(2)).then_inc(l_keys, 1)
                                ve.wait_ge(l_keys, k * 2 + 2)

                            def chunk(q):
                                if not building:
                                    return
                                r = (slot + q) % 2
                                if not (isinstance(k, int) and k * J + q * CH < 2 * CH):
                                    ve.wait_ge(l_built, k * J + (q * CH - CH))
                                ve.tensor_tensor(hi_hot[:, r, :, :], tiles_of(iota_b[:, :], CH), last_dim(hi_g[:, q * CH:(q + 1) * CH], P), ALU.is_equal)
                                for t in range(CH):
                                    last = ve.tensor_scalar(key_hot[:, r, t, :], key_iota, key_g[:, q * CH + t:q * CH + t + 1], None, ALU.is_equal)
                                last.then_inc(l_chunk, 1)

                            chunk(0)
                            chunk(1)
                            if placing:
                                for h in range(2):
                                    ve.tensor_scalar(place_hot[0:HS[h], h, :], iota[0:HS[h], :], place[0:HS[h], h, bass.ds(k - 2, 1)], None, ALU.is_equal)
                                ve.wait_ge(l_slot, k - 1)
                                for h in range(2):
                                    last = ve.tensor_copy(slots[0:HS[h], h, :], slot_ps[0:HS[h], h * D:(h + 1) * D])
                                last.then_inc(l_place, 1)
                            chunk(2)
                            if gathered:
                                ve.wait_ge(l_sum, k)
                                if within(k, 2, NG):
                                    ve.wait_ge(l_acc, k * 2 - 3)
                                window = acc[:, bass.ds(base, W)]
                                ve.tensor_tensor(window, window, agg[:, :], ALU.add).then_inc(l_acc, 1)
                            chunk(3)
                            if placing:
                                first = ve.value_load(first_i[0:1, bass.ds(k - 2, 1)], min_val=0, max_val=N - 1)
                                ve.wait_ge(l_put, k - 1)
                                ve.wait_ge(l_acc, k * 2 - 2)
                                window = acc[0:D, bass.ds(first, W)]
                                ve.tensor_tensor(window, window, put, ALU.add).then_inc(l_acc, 1)
                            chunk(4)
                        each(ve, step, LAST)

                    @block.scalar
                    def _(sc):
                        def step(k, slot, use):
                            if within(k, 0, NC - 1):
                                for t in range(J):
                                    if t == 0 and within(k, 2, NC - 1):
                                        sc.wait_ge(l_applied, k - 1)
                                    sc.wait_ge(l_built, k * J + (t + 1))
                                    sc.activation(
                                        counts[:, slot, :, t * SPAN:(t + 1) * SPAN].rearrange("p (h c) d -> p h c d", h=2),
                                        built[(slot + t) % 2][:, :, 0:HK].rearrange("p h (c d) -> p h c d", d=SPAN),
                                        ACT.Copy).then_inc(l_counts, 1)
                            if within(k, 1, NC):
                                sc.wait_ge(l_applied, k)
                                if within(k, 2, NC):
                                    sc.wait_ge(l_slot, k - 1)
                                sc.activation(prod[:, :], applied[:, :], ACT.Copy).then_inc(l_prod, 1)
                        each(sc, step, LAST)

                    @block.tensor
                    def _(te):
                        def step(k, slot, use):
                            other = 1 - slot
                            other_use = use + slot
                            gathered = within(k, 1, NG)
                            building = within(k, 0, NC - 1)
                            applying = within(k, 1, NC)
                            placing = within(k, 2, NC + 1)
                            if applying:
                                te.wait_ge(l_counts, k * J)
                                if within(k, 2, NC):
                                    te.wait_ge(l_prod, k - 1)
                            for t in range(J):
                                if building:
                                    r = (slot + t // CH) % 2
                                    if t % CH == 0:
                                        te.wait_ge(l_chunk, k * (J // CH) + (t // CH + 1))
                                    if not (isinstance(k, int) and k * J + t < 2):
                                        te.wait_ge(l_counts, k * J + (t - 1))
                                    for h in range(2):
                                        last = te.matmul(built[(slot + t) % 2][:, h, 0:HK], hi_hot[:, r, t % CH, :],
                                                         key_hot[:, r, t % CH, h * HK:(h + 1) * HK], start=True, stop=True)
                                    last.then_inc(l_built, 1)
                                if applying:
                                    for c in range(t * STEPS, min(C, (t + 1) * STEPS)):
                                        last = te.matmul(applied[:, :], x_parts[:, c, :], counts[:, other, c, :], start=(c == 0), stop=(c == C - 1))
                                    if t == J - 1:
                                        last.then_inc(l_applied, 1)
                                if placing and t == 2:
                                    te.wait_ge(l_prod, k - 1)
                                    te.wait_ge(l_acc, k * 2 - 3)
                                    for h in range(2):
                                        last = te.matmul(slot_ps[0:HS[h], h * D:(h + 1) * D], prod[:, h * HS[0]:h * HS[0] + HS[h]],
                                                         fold[:, :], start=True, stop=True)
                                    last.then_inc(l_slot, 1)
                                if gathered and t == 6:
                                    te.wait_ge(l_rows[other], other_use * (16 * J))
                                    te.wait_ge(l_hot, k)
                                    if within(k, 2, NG):
                                        te.wait_ge(l_acc, k * 2 - 3)
                                    for j in range(J):
                                        last = te.matmul(agg[:, :], rows[:, other, j, :], dst_hot[:, j, :], start=(j == 0), stop=(j == J - 1))
                                    last.then_inc(l_sum, 1)
                                if placing and t == 12:
                                    te.wait_ge(l_place, k - 1)
                                    for h in range(2):
                                        last = te.matmul(put, slots[0:HS[h], h, :], place_hot[0:HS[h], h, :], start=(h == 0), stop=(h == 1))
                                    last.then_inc(l_put, 1)
                        each(te, step, LAST)

                general_sums(1, table[:, :], D3, (src_t, dst_t, rows, rel, dst_hot, agg), None, None)

        def general_sums(layer, nodes, M, buffers, edge_t, msg):
            src_t, dst_t, rows, rel, dst_hot, agg = buffers
            v0 = V.n
            g_in, g_rows, g_v, g_a, g_pe = (sem(f"g_{what}{layer}") for what in ("in", "rows", "v", "a", "pe"))
            B = 2 if layer == 0 else 1
            IN = 48 if layer == 0 else 32
            VT = B + 3 * C
            with nc.Block() as block:
                def when_lost(engine):
                    engine.wait_ge(s_v, v0)
                    said = engine.value_load(lost[D:DE, 0:1], min_val=0, max_val=1)
                    if layer == 1:
                        said = said + engine.value_load(lost1[:, :], min_val=0, max_val=1)
                    return engine.If(said > 0)

                @block.sync
                def _(sp):
                    with when_lost(sp):
                        with sp.Fori(0, G) as g:
                            sp.wait_ge(g_v, g * VT + 1)
                            load_indices(sp, g, src_t[:, 0, :], dst_t[:, 0, :], None, g_in)
                            if layer == 0:
                                load_edges(sp, g, edge_t[:, 0, :, :], g_in)

                @block.gpsimd
                def _(gp):
                    with when_lost(gp):
                        with gp.Fori(0, G) as g:
                            gp.wait_ge(g_in, (g + 1) * IN)
                            gp.sem_inc(s_mark, 1)
                            gathers(gp, nodes, rows[:, 0, :, :], src_t[:, 0, :], g_rows)

                @block.vector
                def _(ve):
                    with when_lost(ve):
                        ve.memset(acc[:, :], 0.0).then_inc(g_v, 1)
                        with ve.Fori(0, G) as g:
                            v = g * VT + 1
                            ve.wait_ge(g_in, (g + 1) * IN)
                            ve.tensor_copy(rel[:, :], dst_t[:, 0, :]).then_inc(g_v, 1)
                            if layer == 0:
                                ve.wait_ge(g_rows, (g + 1) * (16 * J))
                                ve.tensor_tensor(edge_t[:, 0, :, :], edge_t[:, 0, :, :], rows[:, 0, :, :], ALU.add).then_inc(g_v, 1)
                            with ve.Fori(0, C) as w:
                                u = v + B + w * 3
                                ve.wait_ge(g_v, u)
                                ve.tensor_tensor(dst_hot[:, :, :], tiles_of(iota[:, :], J), last_dim(rel[:, :], W), ALU.is_equal).then_inc(g_v, 1)
                                ve.wait_ge(g_v, u + 1)
                                ve.tensor_scalar(rel[:, :], rel[:, :], float(W), None, ALU.subtract).then_inc(g_v, 1)
                                ve.wait_ge(g_pe, g * C + w + 1)
                                window = acc[0:M, bass.ds(w * W, W)]
                                ve.tensor_tensor(window, window, agg[0:M, :], ALU.add).then_inc(g_v, 1)

                if layer == 0:
                    @block.scalar
                    def _(sc):
                        with when_lost(sc):
                            with sc.Fori(0, G) as g:
                                sc.wait_ge(g_v, g * VT + 3)
                                sc.activation(msg[:, :, 0:D], edge_t[:, 0, :, :], ACT.Relu).then_inc(g_a, 1)

                @block.tensor
                def _(te):
                    with when_lost(te):
                        with te.Fori(0, G) as g:
                            if layer == 0:
                                te.wait_ge(g_a, g + 1)
                            else:
                                te.wait_ge(g_rows, (g + 1) * (16 * J))
                            te.sem_inc(s_mark, 1)
                            with te.Fori(0, C) as w:
                                te.wait_ge(g_v, g * VT + w * 3 + (B + 2))
                                for j in range(J):
                                    lhs = msg[:, j, :] if layer == 0 else rows[:, 0, j, :]
                                    last = te.matmul(agg[0:M, :], lhs, dst_hot[:, j, :], start=(j == 0), stop=(j == J - 1))
                                last.then_inc(g_pe, 1)

        def to_nodes(layer, sums, turn):
            K, M = (DE, DE) if layer == 0 else (D3, D)
            turner = (ident if layer == 0 else fold)[0:K, 0:M]
            v0, p0 = V.n, PE.n
            with nc.Block() as block:
                @block.tensor
                def _(te):
                    for k in range(C // TR):
                        if k >= 2:
                            te.wait_ge(s_v, v0 + k - 1)
                        for t in range(TR):
                            c = k * TR + t
                            last = te.matmul(turn[k % 2][:, t * M:(t + 1) * M], acc[0:K, c:c + (P - 1) * C + 1:C],
                                             turner, start=True, stop=True)
                        PE(last)

                @block.vector
                def _(ve):
                    for k in range(C // TR):
                        ve.wait_ge(s_pe, p0 + k + 1)
                        V(ve.tensor_copy(sums[:, k * TR:(k + 1) * TR, 0:M],
                                         turn[k % 2][:, 0:TR * M].rearrange("p (t m) -> p t m", m=M)))

        def wide(ap):
            return ap.unsqueeze(2).to_broadcast([P, C, D])

        def finish(layer):
            with ExitStack() as own:
                sb, pb = allocators(own)
                x_n = sb(f"x_n{layer}", [P, C, D])
                sums = sb(f"sums{layer}", [P, C, DE])
                y = sb(f"y{layer}", [P, C, D])
                stat = sb(f"stat{layer}", [P, C])
                var = sb(f"var{layer}", [P, C])
                rstd = sb(f"rstd{layer}", [P, C])
                turn = [pb(f"turn{layer}{k}") for k in range(2)]
                load_nodes(layer, x_n)
                to_nodes(layer, sums, turn)
                norm(layer, x_n, sums, y, stat, var, rstd)

        def load_nodes(layer, x_n):
            with nc.Block() as block:
                if layer == 0:
                    @block.vector
                    def _(ve):
                        V(ve.memset(x_n[:, :, :], 0.0))

                    @block.sync
                    def _(sp):
                        sp.wait_ge(s_v, V.n)
                        sp.dma_start(x_n[0:P - 1, :, :], x[0:(P - 1) * C, :].rearrange("(p c) d -> p c d", c=C)).then_inc(s_x, 16)
                        sp.dma_start(x_n[P - 1:P, 0:TAIL, :], x[(P - 1) * C:N, :].unsqueeze(0)).then_inc(s_x, 16)
                else:
                    @block.sync
                    def _(sp):
                        sp.dma_start(x_n[:, :, :], x1.rearrange("(p c) d -> p c d", c=C)).then_inc(s_x, 16)

        def norm(layer, x_n, sums, y, stat, var, rstd):
            a0, n_x1 = A.n, 0
            sc_steps = []
            with nc.Block() as block:
                @block.vector
                def _(ve):
                    nonlocal n_x1
                    a = [a0]

                    def after(ins):
                        ve.wait_ge(s_v, V(ins))

                    def scalar_step(make):
                        sc_steps.append((V.n, make))
                        a[0] += 1
                        ve.wait_ge(s_a, a[0])

                    agg_n = sums[:, :, 0:D]
                    if layer == 0:
                        ve.wait_ge(s_x, 48)
                        after(ve.tensor_scalar(eps_t[:, :], eps_t[:, :], 1.0, None, ALU.add))
                        after(ve.scalar_tensor_tensor(y[:, :, :], x_n[:, :, :], eps_t[:, 0:1], agg_n, ALU.mult, ALU.add))
                        after(ve.tensor_tensor(y[:, :, :], y[:, :, :], x_n[:, :, :], ALU.add))
                        after(ve.tensor_scalar(r_out[:, :], hist[:, :], 1.0, None, ALU.max))
                        after(ve.tensor_scalar(r_in[:, :], sums[:, :, D], 1.0, None, ALU.max))
                        scalar_step(lambda sc: sc.activation(r_out[:, :], r_out[:, :], ACT.Sqrt))
                        scalar_step(lambda sc: sc.activation(r_in[:, :], r_in[:, :], ACT.Sqrt))
                        after(ve.reciprocal(r_out[:, :], r_out[:, :]))
                        after(ve.reciprocal(r_in[:, :], r_in[:, :]))
                    else:
                        ve.wait_ge(s_x, 64)
                        after(ve.tensor_tensor(y[:, :, :], agg_n, wide(r_in[:, :]), ALU.mult))
                        after(ve.tensor_tensor(y[:, :, :], y[:, :, :], x_n[:, :, :], ALU.add))
                    after(ve.tensor_reduce(stat[:, :], y[:, :, :], AX.X, ALU.add))
                    after(ve.tensor_scalar(stat[:, :], stat[:, :], 1.0 / D, None, ALU.mult))
                    after(ve.tensor_tensor(y[:, :, :], y[:, :, :], wide(stat[:, :]), ALU.subtract))
                    after(ve.tensor_tensor(agg_n, y[:, :, :], y[:, :, :], ALU.mult))
                    after(ve.tensor_reduce(var[:, :], agg_n, AX.X, ALU.add))
                    scalar_step(lambda sc: sc.activation(rstd[:, :], var[:, :], ACT.Sqrt, bias=ln_eps[:, 0:1], scale=1.0 / D))
                    after(ve.reciprocal(rstd[:, :], rstd[:, :]))
                    after(ve.tensor_tensor(x_n[:, :, :], y[:, :, :], wide(rstd[:, :]), ALU.mult))
                    if layer == 0:
                        n_x1 = V.n
                        after(ve.tensor_tensor(y[:, :, :], x_n[:, :, :], wide(r_out[:, :]), ALU.mult))
                        for part in range(PARTS):
                            cut = x_parts[:, :, part * D:(part + 1) * D]
                            after(ve.tensor_copy(cut, y[:, :, :]))
                            if part < PARTS - 1:
                                after(ve.tensor_tensor(y[:, :, :], y[:, :, :], cut, ALU.subtract))
                        V(ve.memset(acc[:, :], 0.0))
                v_done = V.n

                @block.scalar
                def _(sc):
                    for n, make in sc_steps:
                        sc.wait_ge(s_v, n)
                        A(make(sc))

                @block.sync
                def _(sp):
                    if layer == 0:
                        sp.wait_ge(s_v, n_x1)
                        sp.dma_start(x1.rearrange("(p c) d -> p c d", c=C), x_n[:, :, :]).then_inc(s_out, 16)
                        sp.wait_ge(s_v, v_done - 1)
                        sp.dma_start(table.rearrange("(p c) d -> p c d", c=C), x_parts[:, :, :]).then_inc(s_out, 16)
                        sp.wait_ge(s_out, 32)
                    else:
                        sp.wait_ge(s_v, v_done)
                        sp.dma_start(out[0:(P - 1) * C, :].rearrange("(p c) d -> p c d", c=C), x_n[0:P - 1, :, :]).then_inc(s_out, 16)
                        sp.dma_start(out[(P - 1) * C:N, :].unsqueeze(0), x_n[P - 1:P, 0:TAIL, :]).then_inc(s_out, 16)
                        sp.wait_ge(s_out, 64)

        with ExitStack() as first_layer:
            hist = first_layer.enter_context(nc.psum_tensor("hist", [P, 512], F32))[:, 0:C]
            layer_0()
            finish(0)
        layer_1()
        finish(1)


_INS = ['x', 'src', 'dst', 'edge_attr_32', 'L0_gnn_eps']


def kernel(**inputs):
    import numpy as _np
    import concourse.bacc as _bacc
    from concourse import mybir as _mybir
    from concourse.bass_utils import run_bass_kernel_spmd as _run

    nc = _bacc.Bacc("TRN2", target_bir_lowering=False, num_devices=1)
    arrays, args = {}, []
    for name in _INS:
        a = _np.ascontiguousarray(inputs[name])
        arrays[f"in_{name}"] = a
        args.append(nc.dram_tensor(f"in_{name}", a.shape, _mybir.dt.from_np(a.dtype), kind="ExternalInput").ap())
    n, d = inputs['x'].shape
    out = nc.dram_tensor("out", (n, d), _mybir.dt.float32, kind="ExternalOutput").ap()
    padded = -(-n // P) * P
    table = nc.dram_tensor("table", (padded, PARTS * d), _mybir.dt.bfloat16, kind="Internal").ap()
    x1 = nc.dram_tensor("x1", (padded, d), _mybir.dt.float32, kind="Internal").ap()
    build(nc, *args, out, table, x1)
    r = _run(nc, [arrays], core_ids=[0])
    return r.results[0]["out"]
```

```python
import concourse.bass as bass
from concourse import mybir
from contextlib import ExitStack

F32, BF16, F16, I32, U32 = mybir.dt.float32, mybir.dt.bfloat16, mybir.dt.float16, mybir.dt.int32, mybir.dt.uint32
ALU = mybir.AluOpType
ACT = mybir.ActivationFunctionType
AX = mybir.AxisListType

P = 128
PARTS = 3
SPAN = 7
LN_EPS = 1e-5
ROUND = 12582912.0


def build(nc, x, src, dst, edge, eps, out, table, x1):
    N, D = x.shape
    E = src.shape[0]
    J = 25
    GE = P * J
    G = E // GE
    W = P
    C = -(-N // P)
    DE = D + 1
    D3 = PARTS * D
    TAIL = N - (P - 1) * C
    JG = 16
    NG = 3 * J
    NC = G - NG * JG // J
    CE0 = NG * JG * P
    KEYS = C * SPAN
    HK = KEYS // 2
    CH = 5
    HT = [13, J - 13]
    HS = [n * SPAN for n in HT]
    assert G * GE == E and G % 2 == 1 and NC <= P and C % 2 == 0 and CE0 + NC * GE == E and CE0 % GE == 0
    assert 0 < TAIL <= C and HK <= 512 and max(HS) <= P and J % CH == 0 and J - 1 <= C and KEYS <= J * NC

    with ExitStack() as ctx:
        def allocators(stack):
            return (lambda name, shape, dt=F32: stack.enter_context(nc.sbuf_tensor(name, shape, dt)),
                    lambda name: stack.enter_context(nc.psum_tensor(name, [P, 512], F32)))

        sb, pb = allocators(ctx)

        def sem(name):
            return ctx.enter_context(nc.semaphore(name))

        iota_i = sb("iota_i", [P, P], I32)
        iota = sb("iota", [P, P])
        iota_b = sb("iota_b", [P, P], BF16)
        col_i = sb("col_i", [P, 1], I32)
        col = sb("col", [P, 1])
        high = sb("high", [P, 2])
        low = sb("low", [P, 2])
        ident = sb("ident", [P, P])
        fold = sb("fold", [D3, D])
        ones = sb("ones", [P, 1])
        key_iota = sb("key_iota", [P, KEYS], F16)[:, :]
        zero_bf = sb("zero_bf", [P, P], BF16)
        eps_t = sb("eps_t", [P, 1])
        ln_eps = sb("ln_eps", [P, 1])
        acc = sb("acc", [D3, P * C + W])
        r_out = sb("r_out", [P, C])
        r_in = sb("r_in", [P, C])
        x_parts = sb("x_parts", [P, C, D3], BF16)
        hi_all = sb("hi_all", [P, J, NC])
        key_all = sb("key_all", [P, J, NC])
        first_i = sb("first_i", [J, NC], I32)
        first_g = sb("first_g", [1, NG], I32)
        place = sb("place", [max(HS), 2, NC])
        counted = sb("counted", [DE, G])
        count = sb("count", [DE, 1])
        lost = sb("lost", [DE, 1], I32)
        lost1 = sb("lost1", [1, 1], I32)

        s_const = sem("s_const")
        s_x = sem("s_x")
        s_prep = sem("s_prep")
        s_in = [sem(f"s_in{k}") for k in range(2)]
        s_rows = [sem(f"s_rows{k}") for k in range(2)]
        s_late = sem("s_late")
        s_mark = sem("s_mark")
        s_v = sem("s_v")
        s_a = sem("s_a")
        s_pe = sem("s_pe")
        s_gp = sem("s_gp")
        s_agg = sem("s_agg")
        s_out = sem("s_out")

        class Tally:
            def __init__(self, s):
                self.s, self.n = s, 0

            def __call__(self, ins):
                ins.then_inc(self.s, 1)
                self.n += 1
                return self.n

        V, A, PE, GP = Tally(s_v), Tally(s_a), Tally(s_pe), Tally(s_gp)

        def last_dim(ap, n):
            return ap.unsqueeze(2).to_broadcast([ap.shape[0], ap.shape[1], n])

        def tiles_of(ap, n):
            return ap.unsqueeze(1).to_broadcast([P, n, P])

        def load_indices(sp, g, n, src_d, dst_d, base_d, s):
            e0, ne = g * (n * P), n * P
            sp.dma_start(src_d, src[bass.ds(e0, ne)].rearrange("(p j) -> p j", p=P)).then_inc(s, 16)
            sp.dma_start(dst_d, dst[bass.ds(e0, ne)].rearrange("(p j) -> p j", p=P)).then_inc(s, 16)
            if base_d is not None:
                sp.dma_start(base_d, dst[bass.ds(e0, 1)].unsqueeze(0).to_broadcast([P, 1])).then_inc(s, 16)

        def load_edges(sp, g, edge_d, s):
            e0 = g * GE
            sp.dma_start(edge_d.rearrange("p j d -> p (j d)"),
                         edge[bass.ds(e0, GE), :].rearrange("(p j) d -> p (j d)", p=P)).then_inc(s, 16)

        def gathers(gp, j0, j1, nodes, rows_d, src_d, s):
            for j in range(j0, j1):
                gp.indirect_dma_start(
                    rows_d[:, j, :], None, nodes,
                    bass.IndirectOffsetOnAxis(ap=src_d[:, j:j + 1].bitcast(U32), axis=0),
                ).then_inc(s, 16)

        first_layer = ctx.enter_context(ExitStack())
        x_0 = first_layer.enter_context(nc.sbuf_tensor("x_0", [P, C, D], F32))

        keys_i = hi_all[:, :, :].rearrange("p j g -> p (j g)")[:, 0:KEYS].bitcast(I32)
        with nc.Block() as block:
            @block.gpsimd
            def _(gp):
                gp.iota(iota_i[:, :], [[1, P]], base=0, channel_multiplier=0).then_inc(s_const, 1)
                gp.iota(col_i[:, :], [[0, 1]], base=0, channel_multiplier=1).then_inc(s_const, 1)
                gp.iota(keys_i, [[1, KEYS]], base=0, channel_multiplier=0).then_inc(s_const, 1)

            @block.vector
            def _(ve):
                V(ve.memset(zero_bf[:, :], 0.0))
                V(ve.memset(ones[:, :], 1.0))
                V(ve.memset(ln_eps[:, :], LN_EPS))
                ve.wait_ge(s_const, 3)
                V(ve.tensor_copy(key_iota, keys_i))
                V(ve.tensor_copy(iota[:, :], iota_i[:, :]))
                V(ve.tensor_copy(iota_b[:, :], iota_i[:, :]))
                V(ve.tensor_copy(col[:, :], col_i[:, :]))
                for q, m in enumerate((D, SPAN)):
                    n = V(ve.tensor_scalar(high[:, q:q + 1], col_i[:, :], 0.5 - m / 2, 1.0 / m, ALU.add, ALU.mult))
                ve.wait_ge(s_v, n)
                n = V(ve.tensor_scalar(high[:, :], high[:, :], ROUND, ROUND, ALU.add, ALU.subtract))
                V(ve.tensor_scalar(ident[:, :], iota[:, :], col[:, 0:1], None, ALU.is_equal))
                ve.wait_ge(s_v, n)
                for q, m in enumerate((D, SPAN)):
                    n = V(ve.scalar_tensor_tensor(low[:, q:q + 1], high[:, q:q + 1], -float(m), col[:, :], ALU.mult, ALU.add))
                ve.wait_ge(s_v, n)
                V(ve.tensor_scalar(fold[:, :], iota[0:D3, 0:D], low[0:D3, 0:1], None, ALU.is_equal))
        n_const = V.n

        def layer_0():
            turns = G // 2

            def both(engine, step):
                with engine.Fori(0, turns) as i:
                    for slot in range(2):
                        step(i, slot, i * 2 + slot)
                step(turns, 0, G - 1)

            with ExitStack() as own:
                sb, pb = allocators(own)
                src_t = sb("src_t", [P, 2, J], I32)
                dst_t = sb("dst_t", [P, 2, J], I32)
                base_t = sb("base_t", [P, 2, 1], I32)
                edge_t = sb("edge_t", [P, 2, J, D])
                rows = sb("rows", [P, 2, J, D])
                msg = sb("msg", [P, J, DE])
                rel = sb("rel", [P, J])
                quot = sb("quot", [P, J])
                s_hi = sb("s_hi", [P, J])
                s_lo = sb("s_lo", [P, J])
                dst_hot = sb("dst_hot", [P, J, W])
                hi_hot = sb("hi_hot", [P, J, P], BF16)
                lo_hot = sb("lo_hot", [P, J, C], BF16)
                c_dst = sb("c_dst", [NC, J, P], I32)
                c_src = sb("c_src", [NC, J, P], I32)
                c_rel = sb("c_rel", [NC, J, P])
                c_hi = sb("c_hi", [NC, J, P])
                c_key = c_src[:, :, :].bitcast(F32)
                first = sb("first", [J, NC])
                pick_i = sb("pick_i", [J, 2, max(HS)], I32)
                pick = sb("pick", [J, 2, max(HS)])
                is_0 = sb("is_0", [J, 1])
                most = sb("most", [NC, 2])
                bad = sb("bad", [NC, 1])
                agg = pb("agg")[0:DE, 0:W]
                turn = [pb(f"turn{k}") for k in range(2)]
                misc = pb("misc")

                VG = 10
                PIECES = [(0, J - CH), (J - CH, J)]

                TB = 512 // NC
                ROUNDS = [(what, t, min(TB, J - t)) for what in range(2) for t in range(0, J, TB)]

                def prepare_dve(ve):
                    def after(ins):
                        ve.wait_ge(s_v, V(ins))
                    V(ve.memset(x_0[:, :, :], 0.0))
                    V(ve.memset(msg[:, :, D:DE], 1.0))
                    V(ve.memset(acc[:, :], 0.0))
                    ve.wait_ge(s_prep, 64)
                    V(ve.tensor_tensor(c_rel[:, :, :], c_dst[:, :, :], c_dst[:, :, 0:1].to_broadcast([NC, J, P]), ALU.subtract))
                    after(ve.tensor_scalar(c_hi[:, :, :], c_src[:, :, :], 0.5 - C / 2, 1.0 / C, ALU.add, ALU.mult))
                    after(ve.tensor_scalar(c_hi[:, :, :], c_hi[:, :, :], ROUND, ROUND, ALU.add, ALU.subtract))
                    after(ve.scalar_tensor_tensor(c_key, c_hi[:, :, :], -float(C), c_src[:, :, :], ALU.mult, ALU.add))
                    after(ve.scalar_tensor_tensor(c_key, c_key, float(SPAN), c_rel[:, :, :], ALU.mult, ALU.add))
                    n_keys = V.n
                    ve.wait_ge(s_const, 5)
                    V(ve.tensor_copy(first[:, :], first_i[:, :]))
                    V(ve.tensor_scalar(is_0[:, :], col[0:J, :], 0.0, None, ALU.is_equal))
                    after(ve.tensor_scalar(pick[:, :, :], pick_i[:, :, :], col[0:J, 0:1], None, ALU.is_equal))
                    after(ve.tensor_scalar(pick[:, :, :], pick[:, :, :], is_0[:, 0:1], None, ALU.subtract))
                    n_pick = V.n
                    V(ve.tensor_reduce(most[:, 0:1], c_rel[:, :, :], AX.XY, ALU.max))
                    after(ve.tensor_reduce(most[:, 1:2], c_rel[:, :, :], AX.XY, ALU.min))
                    after(ve.tensor_scalar(bad[:, :], most[:, 0:1], float(SPAN - 1), None, ALU.is_gt))
                    after(ve.scalar_tensor_tensor(bad[:, :], most[:, 1:2], 0.0, bad[:, :], ALU.is_lt, ALU.add))
                    n_bad = V.n
                    ve.wait_ge(s_pe, len(ROUNDS) + 1)
                    for h in range(2):
                        V(ve.tensor_scalar(place[0:HS[h], h, :], misc[0:HS[h], h * NC:(h + 1) * NC], low[0:HS[h], 1:2], None, ALU.add))
                    V(ve.tensor_scalar(lost1[:, :], misc[0:1, 2 * NC:2 * NC + 1], 0.0, None, ALU.is_gt))
                    return n_keys, n_pick, n_bad

                def prepare_pe(te):
                    te.wait_ge(s_v, n_keys)
                    for k, (what, t, m) in enumerate(ROUNDS):
                        if k >= 2:
                            te.wait_ge(s_a, k - 1)
                        for q in range(m):
                            turned = (c_hi[:, :, :], c_key)[what][:, t + q, :]
                            last = te.transpose(turn[k % 2][:, q * NC:(q + 1) * NC], turned, ident[0:NC, 0:NC])
                        PE(last)
                    te.wait_ge(s_v, n_bad)
                    for h in range(2):
                        te.matmul(misc[0:HS[h], h * NC:(h + 1) * NC], pick[:, h, 0:HS[h]], first[:, :], start=True, stop=True)
                    PE(te.matmul(misc[0:1, 2 * NC:2 * NC + 1], bad[:, :], ones[0:NC, :], start=True, stop=True))

                with nc.Block() as block:
                    @block.vector
                    def _(ve):
                        nonlocal n_keys, n_bad, v0
                        n_keys, _, n_bad = prepare_dve(ve)
                        v0 = V.n

                        def step(i, slot, g):
                            v = g * VG + v0
                            is_last = isinstance(g, int)
                            ve.wait_ge(s_in[slot], (i + 1) * 64)
                            ve.tensor_scalar(rel[:, :], dst_t[:, slot, :], base_t[:, slot, 0:1], None, ALU.subtract).then_inc(s_v, 1)
                            base = ve.value_load(dst_t[0:1, slot, 0:1], min_val=0, max_val=N - 1)
                            ve.tensor_scalar(quot[:, :], src_t[:, slot, :], 0.5 - C / 2, 1.0 / C, ALU.add, ALU.mult).then_inc(s_v, 1)
                            ve.wait_ge(s_v, v + 2)
                            ve.tensor_scalar(s_hi[:, :], quot[:, :], ROUND, ROUND, ALU.add, ALU.subtract).then_inc(s_v, 1)
                            ve.wait_ge(s_v, v + 3)
                            ve.scalar_tensor_tensor(s_lo[:, :], s_hi[:, :], -float(C), src_t[:, slot, :], ALU.mult, ALU.add).then_inc(s_v, 1)
                            ve.tensor_tensor(hi_hot[:, :, :], tiles_of(iota[:, :], J), last_dim(s_hi[:, :], P), ALU.is_equal).then_inc(s_v, 1)
                            ve.wait_ge(s_v, v + 4)
                            ve.tensor_tensor(lo_hot[:, :, :], tiles_of(iota[:, :], J)[:, :, 0:C], last_dim(s_lo[:, :], C), ALU.is_equal).then_inc(s_v, 1)
                            ve.tensor_tensor(dst_hot[:, :, :], tiles_of(iota[:, :], J), last_dim(rel[:, :], W), ALU.is_equal).then_inc(s_v, 1)
                            for j0, j1 in PIECES if is_last else [(0, J)]:
                                if j0 == 0:
                                    ve.wait_ge(s_rows[slot], i * (16 * J) + 16 * j1)
                                else:
                                    ve.wait_ge(s_late, 16 * (j1 - j0))
                                piece = edge_t[:, slot, j0:j1, :]
                                ve.tensor_tensor(piece, piece, rows[:, slot, j0:j1, :], ALU.add).then_inc(s_v, 1)
                            ve.wait_ge(s_agg, g + 1)
                            window = acc[0:DE, bass.ds(base, W)]
                            ve.tensor_tensor(window, window, agg[:, :], ALU.add).then_inc(s_v, 1)
                            ve.tensor_reduce(counted[D:DE, bass.ds(g, 1)], agg[D:DE, :], AX.X, ALU.add).then_inc(s_v, 1)
                        both(ve, step)
                        V.n += VG * G + len(PIECES) - 1
                        ve.wait_ge(s_v, V.n)
                        n = V(ve.tensor_reduce(count[D:DE, :], counted[D:DE, :], AX.X, ALU.add))
                        ve.wait_ge(s_v, n)
                        V(ve.tensor_scalar(lost[D:DE, :], count[D:DE, :], float(E), None, ALU.not_equal))

                    @block.sync
                    def _(sp):
                        def load(g, slot):
                            load_indices(sp, g, J, src_t[:, slot, :], dst_t[:, slot, :], base_t[:, slot, :], s_in[slot])
                            load_edges(sp, g, edge_t[:, slot, :, :], s_in[slot])

                        for slot in range(2):
                            load(slot, slot)
                        sp.dma_start(c_dst[:, :, :].rearrange("g j p -> g (j p)"), dst[CE0:E].rearrange("(g e) -> g e", e=GE)).then_inc(s_prep, 16)
                        sp.dma_start(c_src[:, :, :].rearrange("g j p -> g (j p)"), src[CE0:E].rearrange("(g e) -> g e", e=GE)).then_inc(s_prep, 16)
                        with nc.allow_non_contiguous_dma(reason="one index of each tile, once"):
                            sp.dma_start(first_i[:, :], dst[CE0:E].rearrange("(g j p) -> j g p", p=P, j=J)[:, :, 0]).then_inc(s_prep, 16)
                            sp.dma_start(first_g[:, :], dst[0:CE0].rearrange("(a g e) -> a g e", a=1, e=JG * P)[:, :, 0]).then_inc(s_prep, 16)
                        sp.dma_start(eps_t[:, :], eps.unsqueeze(0).to_broadcast([P, 1])).then_inc(s_x, 16)
                        sp.wait_ge(s_v, n_const + 1)
                        sp.dma_start(x_0[0:P - 1, :, :], x[0:(P - 1) * C, :].rearrange("(p c) d -> p c d", c=C)).then_inc(s_x, 16)
                        sp.dma_start(x_0[P - 1:P, 0:TAIL, :], x[(P - 1) * C:N, :].unsqueeze(0)).then_inc(s_x, 16)

                        def refill(i, slot, g):
                            sp.wait_ge(s_a, g + (len(ROUNDS) + 1))
                            load(g + 2, slot)
                        with sp.Fori(0, turns - 1) as i:
                            for slot in range(2):
                                refill(i, slot, i * 2 + slot)
                        refill(turns - 1, 0, G - 3)

                    @block.gpsimd
                    def _(gp):
                        for h in range(2):
                            gp.iota(pick_i[:, h, :], [[1, max(HT)], [0, SPAN]], base=h * HT[0], channel_multiplier=0).then_inc(s_const, 1)

                        def step(i, slot, g):
                            gp.wait_ge(s_in[slot], (i + 1) * 64)
                            gp.sem_inc(s_mark, 1)
                            n = PIECES[0][1] if isinstance(g, int) else J
                            gathers(gp, 0, n, x[:, :], rows[:, slot, :, :], src_t[:, slot, :], s_rows[slot])
                            if n < J:
                                gathers(gp, n, J, x[:, :], rows[:, slot, :, :], src_t[:, slot, :], s_late)
                        both(gp, step)

                    @block.scalar
                    def _(sc):
                        for k, (what, t, m) in enumerate(ROUNDS):
                            sc.wait_ge(s_pe, k + 1)
                            A(sc.activation((hi_all, key_all)[what][:, t:t + m, :],
                                            turn[k % 2][:, 0:m * NC].rearrange("p (t g) -> p t g", g=NC), ACT.Copy))

                        def step(i, slot, g):
                            for n, (j0, j1) in enumerate(PIECES if isinstance(g, int) else [(0, J)]):
                                sc.wait_ge(s_v, g * VG + (v0 + 8 + n))
                                sc.activation(msg[:, j0:j1, 0:D], edge_t[:, slot, j0:j1, :], ACT.Relu).then_inc(s_a, 1)
                        both(sc, step)

                    @block.tensor
                    def _(te):
                        te.wait_ge(s_v, n_const)
                        te.matmul(hist[:, :], zero_bf[:, :], zero_bf[:, 0:C], start=True, stop=False)
                        prepare_pe(te)

                        def step(i, slot, g):
                            te.wait_ge(s_v, g * VG + (v0 + 6))
                            for j in range(J):
                                te.matmul(hist[:, :], hi_hot[:, j, :], lo_hot[:, j, :], start=False, stop=False)
                            for n, (j0, j1) in enumerate(PIECES if isinstance(g, int) else [(0, J)]):
                                te.wait_ge(s_a, g + (len(ROUNDS) + 1 + n))
                                for j in range(j0, j1):
                                    last = te.matmul(agg[:, :], msg[:, j, :], dst_hot[:, j, :], start=(j == 0), stop=(j == J - 1))
                            last.then_inc(s_agg, 1)
                        both(te, step)
                        PE(te.matmul(hist[:, :], zero_bf[:, :], zero_bf[:, 0:C], start=False, stop=True))

                A.n += G + len(PIECES) - 1
                general_sums(0, x[:, :], J, DE, (src_t, dst_t, rows, rel, dst_hot, agg), edge_t, msg)

        n_keys = n_bad = v0 = 0

        def layer_1():
            LAST = max(NC + 1, NG)
            pairs = min(NC, NG) // 2 - 1

            def each(engine, step, last):
                step(0, 0, 0)
                step(1, 1, 0)
                with engine.Fori(0, pairs) as i:
                    for slot in range(2):
                        step(i * 2 + (2 + slot), slot, i + 1)
                for k in range(2 + 2 * pairs, last + 1):
                    step(k, k % 2, k // 2)

            def within(k, lo, hi):
                return not isinstance(k, int) or lo <= k <= hi

            with ExitStack() as own:
                sb, pb = allocators(own)
                src_t = sb("src_1", [P, 2, JG], I32)
                dst_t = sb("dst_1", [P, 2, JG], I32)
                base_t = sb("base_1", [P, 2, 1], I32)
                rows = sb("rows_1", [P, 2, JG, D3], BF16)
                rel = sb("rel_1", [P, JG])
                dst_hot = sb("dst_hot_1", [P, JG, W], BF16)
                reach = sb("reach", [P, 2, NG])
                ends = sb("ends", [P, 2])
                outside = sb("outside", [P, 1])
                hi_g = sb("hi_g", [P, 2, J])
                key_g = sb("key_g", [P, 2, J])
                hi_hot = sb("hi_hot_1", [P, 2, CH, P], BF16)
                key_hot = sb("key_hot", [P, 2, CH, KEYS], BF16)
                counts = sb("counts", [P, 2, C, J * SPAN], BF16)
                prod = sb("prod", [D3, J * SPAN])
                slots = sb("slots", [max(HS), 2, D])
                place_hot = sb("place_hot", [max(HS), 2, W])
                built = [own.enter_context(nc.psum_tensor(f"built{k}", [P, 2, 512], F32)) for k in range(3)]
                applied = pb("applied")[0:D3, 0:J * SPAN]
                shared = pb("shared")
                agg = shared[0:D3, 0:W]
                small = shared[:, W:512]
                slot_ps = small[0:max(HS), 0:2 * D]
                put = small[0:D, 2 * D:2 * D + W]

                l_in = [sem(f"l_in{k}") for k in range(2)]
                l_rows = [sem(f"l_rows{k}") for k in range(2)]
                l_hot = sem("l_hot")
                l_rel = sem("l_rel")
                l_keys = sem("l_keys")
                l_chunk = sem("l_chunk")
                l_place = sem("l_place")
                l_added = sem("l_added")
                l_moved = sem("l_moved")
                l_sum = sem("l_sum")
                l_built = sem("l_built")
                l_applied = sem("l_applied")
                l_slot = sem("l_slot")
                l_put = sem("l_put")
                l_counts = sem("l_counts")
                l_reach = sem("l_reach")
                l_prod = sem("l_prod")

                RING = [t % 3 for t in range(J - 1)] + [1]

                def since(t):
                    return next(d for d in range(1, J) if RING[(t - d) % J] == RING[t])

                def counts_of(slot, t):
                    return (counts[:, slot, :, t * SPAN:(t + 1) * SPAN].rearrange("p (h c) d -> p h c d", h=2),
                            built[RING[t]][:, :, 0:HK].rearrange("p h (c d) -> p h c d", d=SPAN))

                with nc.Block() as block:
                    @block.sync
                    def _(sp):
                        def step(g, slot, use):
                            if within(g, 2, NG):
                                sp.wait_ge(l_rows[slot], use * (16 * JG))
                                sp.wait_ge(l_hot, g - 1)
                            load_indices(sp, g, JG, src_t[:, slot, :], dst_t[:, slot, :], base_t[:, slot, :], l_in[slot])
                        each(sp, step, NG - 1)

                    @block.gpsimd
                    def _(gp):
                        def step(g, slot, use):
                            gp.wait_ge(l_in[slot], (use + 1) * 48)
                            gp.sem_inc(s_mark, 1)
                            if within(g, 2, NG):
                                gp.wait_ge(l_sum, g - 1)
                                gp.sem_inc(s_mark, 1)
                            gathers(gp, 0, JG, table[:, :], rows[:, slot, :, :], src_t[:, slot, :], l_rows[slot])
                        each(gp, step, NG - 1)

                    @block.vector
                    def _(ve):
                        ve.sem_inc(l_moved, 1)

                        def step(k, slot, use):
                            hot = within(k, 0, NG - 1)
                            adding = within(k, 1, NG)
                            building = within(k, 0, NC - 1)
                            placing = within(k, 2, NC + 1)
                            HJ = JG // 2

                            def dst_hots(j0, j1):
                                return ve.tensor_tensor(dst_hot[:, j0:j1, :], tiles_of(iota_b[:, :], j1 - j0),
                                                        last_dim(rel[:, j0:j1], W), ALU.is_equal)

                            def chunk(q):
                                if not building:
                                    return
                                r = (slot + q) % 2
                                if not (isinstance(k, int) and k * J + q * CH < 2 * CH):
                                    ve.wait_ge(l_built, k * J + (q * CH - CH))
                                ve.tensor_tensor(hi_hot[:, r, :, :], tiles_of(iota_b[:, :], CH), last_dim(hi_g[:, slot, q * CH:(q + 1) * CH], P), ALU.is_equal)
                                for t in range(CH):
                                    last = ve.tensor_scalar(key_hot[:, r, t, :], key_iota, key_g[:, slot, q * CH + t:q * CH + t + 1], None, ALU.is_equal)
                                last.then_inc(l_chunk, 1)

                            if building:
                                ve.tensor_copy(hi_g[:, slot, :], hi_all[:, :, bass.ds(k, 1)].squeeze(2)).then_inc(l_keys, 1)
                                ve.tensor_copy(key_g[:, slot, :], key_all[:, :, bass.ds(k, 1)].squeeze(2)).then_inc(l_keys, 1)
                                ve.wait_ge(l_keys, k * 2 + 2)
                            chunk(0)
                            if hot:
                                if within(k, 1, NG - 1):
                                    ve.wait_ge(l_hot, k)
                                ve.wait_ge(l_in[slot], (use + 1) * 48)
                                ve.tensor_scalar(rel[:, :], dst_t[:, slot, :], base_t[:, slot, 0:1], None, ALU.subtract).then_inc(l_rel, 1)
                            chunk(1)
                            if adding:
                                base = ve.value_load(first_g[0:1, bass.ds(k - 1, 1)], min_val=0, max_val=N - 1)
                                ve.wait_ge(l_sum, k)
                                if within(k, 2, NG):
                                    ve.wait_ge(l_moved, k - 1)
                                window = acc[:, bass.ds(base, W)]
                                ve.tensor_tensor(window, window, agg[:, :], ALU.add).then_inc(l_added, 1)
                            if hot:
                                ve.wait_ge(l_rel, k + 1)
                                ve.tensor_reduce(reach[:, 0:1, bass.ds(k, 1)].squeeze(2), rel[:, :], AX.X, ALU.max).then_inc(l_reach, 1)
                                ve.tensor_reduce(reach[:, 1:2, bass.ds(k, 1)].squeeze(2), rel[:, :], AX.X, ALU.min).then_inc(l_reach, 1)
                            if hot:
                                dst_hots(0, HJ)
                            chunk(2)
                            if placing:
                                for h in range(2):
                                    ve.tensor_scalar(place_hot[0:HS[h], h, :], iota[0:HS[h], :], place[0:HS[h], h, bass.ds(k - 2, 1)], None, ALU.is_equal)
                                ve.wait_ge(l_slot, k - 1)
                                for h in range(2):
                                    last = ve.tensor_copy(slots[0:HS[h], h, :], slot_ps[0:HS[h], h * D:(h + 1) * D])
                                last.then_inc(l_place, 1)
                            chunk(3)
                            if hot:
                                dst_hots(HJ, JG).then_inc(l_hot, 1)
                            chunk(4)
                            if placing:
                                first = ve.value_load(first_i[0:1, bass.ds(k - 2, 1)], min_val=0, max_val=N - 1)
                                ve.wait_ge(l_put, k - 1)
                                ve.wait_ge(l_added, k if within(k, 2, NG) else NG)
                                window = acc[0:D, bass.ds(first, W)]
                                ve.tensor_tensor(window, window, put, ALU.add).then_inc(l_moved, 1)
                        each(ve, step, LAST)
                        ve.wait_ge(l_reach, 2 * NG)
                        V(ve.tensor_reduce(ends[:, 0:1], reach[:, 0, :], AX.X, ALU.max))
                        ve.wait_ge(s_v, V(ve.tensor_reduce(ends[:, 1:2], reach[:, 1, :], AX.X, ALU.min)))
                        ve.wait_ge(s_v, V(ve.tensor_scalar(outside[:, :], ends[:, 0:1], float(W - 1), None, ALU.is_gt)))
                        V(ve.scalar_tensor_tensor(outside[:, :], ends[:, 1:2], 0.0, outside[:, :], ALU.is_lt, ALU.add))
                        ve.wait_ge(s_pe, PE.n + 1)
                        V(ve.scalar_tensor_tensor(lost1[:, :], small[0:1, 0:1], 0.0, lost1[:, :], ALU.is_gt, ALU.max))

                    @block.scalar
                    def _(sc):
                        def step(k, slot, use):
                            if within(k, 0, NC - 1):
                                for t in range(J):
                                    if t == 0 and within(k, 2, NC - 1):
                                        sc.wait_ge(l_applied, k - 1)
                                    sc.wait_ge(l_built, k * J + (t + 1))
                                    sc.activation(*counts_of(slot, t), ACT.Copy).then_inc(l_counts, 1)
                            if within(k, 1, NC):
                                sc.wait_ge(l_applied, k)
                                if within(k, 2, NC):
                                    sc.wait_ge(l_slot, k - 1)
                                sc.activation(prod[:, :], applied[:, :], ACT.Copy).then_inc(l_prod, 1)
                        each(sc, step, LAST)

                    @block.tensor
                    def _(te):
                        def step(k, slot, use):
                            other = 1 - slot
                            other_use = use + slot
                            gathered = within(k, 1, NG)
                            building = within(k, 0, NC - 1)
                            applying = within(k, 1, NC)
                            placing = within(k, 2, NC + 1)
                            for t in range(J):
                                if building:
                                    r = (slot + t // CH) % 2
                                    if t % CH == 0:
                                        te.wait_ge(l_chunk, k * (J // CH) + (t // CH + 1))
                                    if not (isinstance(k, int) and k * J + t < since(t)):
                                        te.wait_ge(l_counts, k * J + (t + 1 - since(t)))
                                    for h in range(2):
                                        last = te.matmul(built[RING[t]][:, h, 0:HK], hi_hot[:, r, t % CH, :],
                                                         key_hot[:, r, t % CH, h * HK:(h + 1) * HK], start=True, stop=True)
                                    last.then_inc(l_built, 1)
                                if gathered and t == 0:
                                    te.wait_ge(l_rows[other], other_use * (16 * JG))
                                    te.wait_ge(l_hot, k)
                                    if within(k, 2, NG):
                                        te.wait_ge(l_added, k - 1)
                                        te.wait_ge(l_moved, k - 1)
                                    for j in range(JG):
                                        last = te.matmul(agg[:, :], rows[:, other, j, :], dst_hot[:, j, :], start=(j == 0), stop=(j == JG - 1))
                                    last.then_inc(l_sum, 1)
                                if applying and t > 0:
                                    if t == 1:
                                        te.wait_ge(l_counts, k * J)
                                        if within(k, 2, NC):
                                            te.wait_ge(l_prod, k - 1)
                                    for c in range(C * (t - 1) // (J - 1), C * t // (J - 1)):
                                        last = te.matmul(applied[:, :], x_parts[:, c, :], counts[:, other, c, :], start=(c == 0), stop=(c == C - 1))
                                    if t == J - 1:
                                        last.then_inc(l_applied, 1)
                                if placing and t == 7:
                                    te.wait_ge(l_prod, k - 1)
                                    te.wait_ge(l_added, k if gathered else NG)
                                    te.wait_ge(l_moved, k - 1)
                                    for h in range(2):
                                        last = te.matmul(slot_ps[0:HS[h], h * D:(h + 1) * D], prod[:, h * HS[0]:h * HS[0] + HS[h]],
                                                         fold[:, :], start=True, stop=True)
                                    last.then_inc(l_slot, 1)
                                if placing and t == 18:
                                    te.wait_ge(l_place, k - 1)
                                    for h in range(2):
                                        last = te.matmul(put, slots[0:HS[h], h, :], place_hot[0:HS[h], h, :], start=(h == 0), stop=(h == 1))
                                    last.then_inc(l_put, 1)
                        each(te, step, LAST)
                        te.wait_ge(s_v, V.n - 1)
                        PE(te.matmul(small[0:1, 0:1], outside[:, :], ones[:, :], start=True, stop=True))


                general_sums(1, table[:, :], CH, D3, (src_t, dst_t, rows, rel, dst_hot, agg), None, None)

        def general_sums(layer, nodes, n, M, buffers, edge_t, msg):
            groups = E // (n * P)
            assert groups * n * P == E
            src_t, dst_t, rows, rel, dst_hot, agg = buffers
            v0 = V.n
            g_in, g_rows, g_v, g_a, g_pe = (sem(f"g_{what}{layer}") for what in ("in", "rows", "v", "a", "pe"))
            B = 2 if layer == 0 else 1
            IN = 48 if layer == 0 else 32
            VT = B + 3 * C
            with nc.Block() as block:
                def when_lost(engine):
                    engine.wait_ge(s_v, v0)
                    said = engine.value_load(lost[D:DE, 0:1], min_val=0, max_val=1)
                    if layer == 1:
                        said = said + engine.value_load(lost1[:, :], min_val=0, max_val=1)
                    return engine.If(said > 0)

                @block.sync
                def _(sp):
                    with when_lost(sp):
                        with sp.Fori(0, groups) as g:
                            sp.wait_ge(g_v, g * VT + 1)
                            load_indices(sp, g, n, src_t[:, 0, 0:n], dst_t[:, 0, 0:n], None, g_in)
                            if layer == 0:
                                load_edges(sp, g, edge_t[:, 0, :, :], g_in)

                @block.gpsimd
                def _(gp):
                    with when_lost(gp):
                        with gp.Fori(0, groups) as g:
                            gp.wait_ge(g_in, (g + 1) * IN)
                            gp.sem_inc(s_mark, 1)
                            gathers(gp, 0, n, nodes, rows[:, 0, :, :], src_t[:, 0, :], g_rows)

                @block.vector
                def _(ve):
                    with when_lost(ve):
                        ve.memset(acc[:, :], 0.0).then_inc(g_v, 1)
                        with ve.Fori(0, groups) as g:
                            v = g * VT + 1
                            ve.wait_ge(g_in, (g + 1) * IN)
                            ve.tensor_copy(rel[:, 0:n], dst_t[:, 0, 0:n]).then_inc(g_v, 1)
                            if layer == 0:
                                ve.wait_ge(g_rows, (g + 1) * (16 * n))
                                ve.tensor_tensor(edge_t[:, 0, :, :], edge_t[:, 0, :, :], rows[:, 0, :, :], ALU.add).then_inc(g_v, 1)
                            with ve.Fori(0, C) as w:
                                u = v + B + w * 3
                                ve.wait_ge(g_v, u)
                                ve.tensor_tensor(dst_hot[:, 0:n, :], tiles_of(iota[:, :], n), last_dim(rel[:, 0:n], W), ALU.is_equal).then_inc(g_v, 1)
                                ve.wait_ge(g_v, u + 1)
                                ve.tensor_scalar(rel[:, 0:n], rel[:, 0:n], float(W), None, ALU.subtract).then_inc(g_v, 1)
                                ve.wait_ge(g_pe, g * C + w + 1)
                                window = acc[0:M, bass.ds(w * W, W)]
                                ve.tensor_tensor(window, window, agg[0:M, :], ALU.add).then_inc(g_v, 1)

                if layer == 0:
                    @block.scalar
                    def _(sc):
                        with when_lost(sc):
                            with sc.Fori(0, groups) as g:
                                sc.wait_ge(g_v, g * VT + 3)
                                sc.activation(msg[:, :, 0:D], edge_t[:, 0, :, :], ACT.Relu).then_inc(g_a, 1)

                @block.tensor
                def _(te):
                    with when_lost(te):
                        with te.Fori(0, groups) as g:
                            if layer == 0:
                                te.wait_ge(g_a, g + 1)
                            else:
                                te.wait_ge(g_rows, (g + 1) * (16 * n))
                            te.sem_inc(s_mark, 1)
                            with te.Fori(0, C) as w:
                                te.wait_ge(g_v, g * VT + w * 3 + (B + 2))
                                for j in range(n):
                                    lhs = msg[:, j, :] if layer == 0 else rows[:, 0, j, :]
                                    last = te.matmul(agg[0:M, :], lhs, dst_hot[:, j, :], start=(j == 0), stop=(j == n - 1))
                                last.then_inc(g_pe, 1)

        def in_steps(steps, loaded):
            tallies = {"vector": V, "scalar": A, "tensor": PE, "gpsimd": GP}
            done, ahead = dict(loaded), {engine: t.n for engine, t in tallies.items()}
            for engine, name, _, _ in steps:
                if engine in tallies:
                    ahead[engine] += 1
                    done[name] = (tallies[engine].s, ahead[engine])
            with nc.Block() as block:
                for engine, register in (("vector", block.vector), ("scalar", block.scalar),
                                         ("tensor", block.tensor), ("gpsimd", block.gpsimd), ("sync", block.sync)):
                    mine = [step for step in steps if step[0] == engine]
                    if not mine:
                        continue

                    @register
                    def _(eng, mine=mine, engine=engine):
                        for _, name, after, issue in mine:
                            for a in after:
                                eng.wait_ge(*done[a])
                            if engine in tallies:
                                tallies[engine](issue(eng))
                            else:
                                issue(eng)

        def finish(layer, x_n):
            K, TC = (DE, 14) if layer == 0 else (D3, 5)
            rounds = [(c, min(TC, C - c)) for c in range(0, C, TC)]
            CUT = -(-len(rounds) // 2)
            with ExitStack() as own:
                sb, pb = allocators(own)
                y = sb(f"y{layer}", [P, C, D])
                sq = sb(f"sq{layer}", [P, C, D])
                stat = sb(f"stat{layer}", [P, C])
                var = sb(f"var{layer}", [P, C])
                rstd = sb(f"rstd{layer}", [P, C])
                scale = sb(f"scale{layer}", [P, C])
                turn = [pb(f"turn{layer}{k}") for k in range(4)]
                steps, loaded = [], {}

                def add(engine, name, after, issue):
                    steps.append((engine, name, after, issue))

                def turned(te, k):
                    c0, n = rounds[k]
                    for t in range(n):
                        c = c0 + t
                        last = te.transpose(turn[k % 4][:, t * K:(t + 1) * K], acc[0:K, c:c + (P - 1) * C + 1:C], ident[0:K, 0:K])
                    return last

                def round_steps(k):
                    c0, n = rounds[k]
                    bank = turn[k % 4][:, 0:n * K]
                    y_k, x_k, r_k = y[:, c0:c0 + n, :], x_n[:, c0:c0 + n, :], r_in[:, c0:c0 + n]
                    if layer == 0:
                        bank = bank.rearrange("p (t m) -> p t m", m=K)
                        return [("vector", f"y {k}", [f"turned {k}", "eps"], lambda ve: ve.scalar_tensor_tensor(
                                    y_k, x_k, eps_t[:, 0:1], bank[:, :, 0:D], ALU.mult, ALU.add)),
                                ("vector", f"used {k}", [], lambda ve: ve.tensor_scalar(r_k, bank[:, :, D], 1.0, None, ALU.max))]
                    return [("vector", f"used {k}", [f"turned {k}"], lambda ve: ve.tensor_reduce(
                                y_k, bank.rearrange("p (t a f) -> p t f a", a=PARTS, f=D), AX.X, ALU.add))]

                for k in range(len(rounds)):
                    add("tensor", f"turned {k}", [f"used {k - 4}"] if k >= 4 else [], lambda te, k=k: turned(te, k))

                cut = rounds[CUT][0]
                parts = [(0, cut, CUT - 1), (cut, C, len(rounds) - 1)]
                queues = []
                for h, (c0, c1, last_round) in enumerate(parts):
                    def wide(ap, c0=c0, c1=c1):
                        return ap[:, c0:c1].unsqueeze(2).to_broadcast([P, c1 - c0, D])

                    def of(t, c0=c0, c1=c1):
                        return t[:, c0:c1, 0:D]

                    def cols(t, c0=c0, c1=c1):
                        return t[:, c0:c1]

                    q = []

                    def step(engine, name, after, issue, h=h, q=q):
                        q.append((engine, f"{name} {'ab'[h]}", [f"{a} {'ab'[h]}" if isinstance(a, str) else f"{a[0]}" for a in after], issue))

                    for k in range(h * CUT, last_round + 1):
                        q.extend(round_steps(k))
                    last_sums = (f"used {last_round}",)
                    if layer == 0:
                        step("vector", "out", [], lambda ve, cols=cols: ve.tensor_scalar(cols(r_out), cols(hist), 1.0, None, ALU.max))
                        step("scalar", "root out", ["out"], lambda sc, cols=cols: sc.activation(cols(r_out), cols(r_out), ACT.Sqrt))
                        step("scalar", "root in", [last_sums], lambda sc, cols=cols: sc.activation(cols(r_in), cols(r_in), ACT.Sqrt))
                    else:
                        step("vector", "normed", [last_sums], lambda ve, of=of, wide=wide: ve.tensor_tensor(of(y), of(y), wide(r_in), ALU.mult))
                        step("vector", "y", ["normed", ("x_n",)], lambda ve, of=of: ve.tensor_tensor(of(y), of(y), of(x_n), ALU.add))
                    step("vector", "total", [last_sums] if layer == 0 else ["y"], lambda ve, of=of, cols=cols: ve.tensor_reduce(cols(stat), of(y), AX.X, ALU.add))
                    step("vector", "mean", ["total"], lambda ve, cols=cols: ve.tensor_scalar(cols(stat), cols(stat), 1.0 / D, None, ALU.mult))
                    step("vector", "centred", ["mean"], lambda ve, of=of, wide=wide: ve.tensor_tensor(of(y), of(y), wide(stat), ALU.subtract))
                    step("scalar", "squares", ["centred"], lambda sc, of=of: sc.activation(of(sq), of(y), ACT.Square))
                    step("vector", "var", ["squares"], lambda ve, of=of, cols=cols: ve.tensor_reduce(cols(var), of(sq), AX.X, ALU.add))
                    step("scalar", "deviation", ["var"], lambda sc, cols=cols: sc.activation(
                        cols(rstd), cols(var), ACT.Sqrt, bias=ln_eps[:, 0:1], scale=1.0 / D))
                    step("vector", "rstd", ["deviation"], lambda ve, cols=cols: ve.reciprocal(cols(rstd), cols(rstd)))
                    if layer == 0:
                        step("vector", "r_out", ["root out"], lambda ve, cols=cols: ve.reciprocal(cols(r_out), cols(r_out)))
                        step("vector", "r_in", ["root in"], lambda ve, cols=cols: ve.reciprocal(cols(r_in), cols(r_in)))
                        step("vector", "scale", ["rstd", "r_out"], lambda ve, cols=cols: ve.tensor_tensor(cols(scale), cols(rstd), cols(r_out), ALU.mult))
                        step("vector", "left 0", ["scale"], lambda ve, of=of, wide=wide: ve.tensor_tensor(of(sq), of(y), wide(scale), ALU.mult))
                        for n in range(PARTS):
                            def cut(c0=c0, c1=c1, n=n):
                                return x_parts[:, c0:c1, n * D:(n + 1) * D]
                            step("scalar", f"part {n}", [f"left {n}"], lambda sc, of=of, cut=cut: sc.activation(cut(), of(sq), ACT.Copy))
                            if n < PARTS - 1:
                                step("vector", f"left {n + 1}", [f"part {n}"], lambda ve, of=of, cut=cut: ve.tensor_tensor(of(sq), of(sq), cut(), ALU.subtract))
                        step("sync", "table", [f"part {PARTS - 1}"], lambda sp, c0=c0, c1=c1: sp.dma_start(
                            table.rearrange("(p c) d -> p c d", c=C)[:, c0:c1, :], x_parts[:, c0:c1, :]).then_inc(s_out, 16))
                    step("vector", "output", ["rstd"], lambda ve, of=of, wide=wide: ve.tensor_tensor(of(x_n), of(y), wide(rstd), ALU.mult))
                    if layer == 0:
                        step("sync", "kept", ["output"], lambda sp, c0=c0, c1=c1: sp.dma_start(
                            x1.rearrange("(p c) d -> p c d", c=C)[:, c0:c1, :], x_n[:, c0:c1, :]).then_inc(s_out, 16))
                    else:
                        step("sync", "stored", ["output"], lambda sp, c0=c0, c1=c1: sp.dma_start(
                            out[0:(P - 1) * C, :].rearrange("(p c) d -> p c d", c=C)[:, c0:c1, :], x_n[0:P - 1, c0:c1, :]).then_inc(s_out, 16))
                        if c0 < TAIL:
                            step("sync", "last stored", [], lambda sp, c0=c0, c1=min(c1, TAIL): sp.dma_start(
                                out[(P - 1) * C + c0:(P - 1) * C + c1, :].unsqueeze(0), x_n[P - 1:P, c0:c1, :]).then_inc(s_out, 16))
                    queues.append(q)

                if layer == 0:
                    def ready(ve):
                        ve.wait_ge(s_x, 48)
                        return ve.tensor_scalar(eps_t[:, :], eps_t[:, :], 2.0, None, ALU.add)
                    add("vector", "eps", [], ready)
                    add("gpsimd", "cleared", [f"turned {len(rounds) - 1}"], lambda gp: gp.memset(acc[:, :], 0.0))
                else:
                    add("sync", "x_n", [], lambda sp: sp.dma_start(x_n[:, :, :], x1.rearrange("(p c) d -> p c d", c=C)).then_inc(s_x, 16))

                    loaded["x_n"] = (s_x, 64)
                first, second = queues
                ahead = sum(len(round_steps(k)) for k in range(CUT))
                steps += first[:ahead]
                del first[:ahead]
                while first or second:
                    steps += first[:1] + second[:1]
                    del first[:1], second[:1]
                stores = sum(engine == "sync" and name != "x_n" for engine, name, _, _ in steps)
                stored[0] += 16 * stores

                def all_stored(sp, n=stored[0]):
                    sp.wait_ge(s_out, n)
                add("sync", "all stored", [], all_stored)
                in_steps(steps, loaded)

        stored = [0]
        hist = first_layer.enter_context(nc.psum_tensor("hist", [P, 512], F32))[:, 0:C]
        layer_0()
        finish(0, x_0)
        first_layer.close()
        layer_1()
        with nc.sbuf_tensor("x_1", [P, C, D], F32) as x_1:
            finish(1, x_1)


_INS = ['x', 'src', 'dst', 'edge_attr_32', 'L0_gnn_eps']


def kernel(**inputs):
    import numpy as _np
    import concourse.bacc as _bacc
    from concourse import mybir as _mybir
    from concourse.bass_utils import run_bass_kernel_spmd as _run

    nc = _bacc.Bacc("TRN2", target_bir_lowering=False, num_devices=1)
    arrays, args = {}, []
    for name in _INS:
        a = _np.ascontiguousarray(inputs[name])
        arrays[f"in_{name}"] = a
        args.append(nc.dram_tensor(f"in_{name}", a.shape, _mybir.dt.from_np(a.dtype), kind="ExternalInput").ap())
    n, d = inputs['x'].shape
    out = nc.dram_tensor("out", (n, d), _mybir.dt.float32, kind="ExternalOutput").ap()
    padded = -(-n // P) * P
    table = nc.dram_tensor("table", (padded, PARTS * d), _mybir.dt.bfloat16, kind="Internal").ap()
    x1 = nc.dram_tensor("x1", (padded, d), _mybir.dt.float32, kind="Internal").ap()
    build(nc, *args, out, table, x1)
    r = _run(nc, [arrays], core_ids=[0])
    return r.results[0]["out"]
```
